# Optimizing a Trainium2 kernel written in Bass

```python
import numpy as np
import jax
import jax.numpy as jnp

def _softmax(x, axis=-1):
    return jax.nn.softmax(x, axis=axis)
def _gelu(x):
    return jax.nn.gelu(x, approximate=True)
def _silu(x):
    return jax.nn.silu(x)
def _sigmoid(x):
    return jax.nn.sigmoid(x)
def _layernorm(x, axis=-1, eps=1e-5):
    m = jnp.mean(x, axis=axis, keepdims=True)
    v = jnp.var(x, axis=axis, keepdims=True)
    return (x - m) / jnp.sqrt(v + eps)
def _scatter_add(tgt, idx, src, axis=0):
    return tgt.at[idx].add(src)
def _segment_sum(src, seg, n):
    return jax.ops.segment_sum(src, seg, n)

kernel_name = 'mk_conv_preact_d1_conv_nchw256_ec19a6'

def setup_inputs(seed: int = 0):
    np.random.seed(seed)
    _w = jnp.asarray
    def _rec_inputs():
        import jax
        import jax.numpy as jnp
        _gk = jax.random.key(seed)
        x = -0.0002422 + 1 * jax.random.normal(jax.random.fold_in(_gk, 1), (16, 256, 80, 80), jnp.float32)
        return x
    x = _rec_inputs()
    def _L0_conv_setup():
        import jax, jax.numpy as jnp
        import numpy as np
        NUM_HEADS = 8
        key = jax.random.key(seed)
        ks = jax.random.split(key, 6)
        B, C, H, W = (16, 256, 80, 80)
        N = H * W
        x = jax.random.normal(ks[0], (B, C, H, W), dtype=jnp.float32)
        qkv_w = jax.random.normal(ks[1], (3 * C, C), dtype=jnp.float32) * C ** (-0.5)
        qkv_b = jax.random.normal(ks[2], (3 * C,), dtype=jnp.float32) * 0.02
        pos_enc = jax.random.normal(ks[3], (1, N, C), dtype=jnp.float32) * 0.02
        proj_w = jax.random.normal(ks[4], (C, C), dtype=jnp.float32) * C ** (-0.5)
        proj_b = jax.random.normal(ks[5], (C,), dtype=jnp.float32) * 0.02
        return {'x': x, 'qkv_w': qkv_w, 'qkv_b': qkv_b, 'pos_enc': pos_enc, 'proj_w': proj_w, 'proj_b': proj_b}
    _L0_conv_all = _L0_conv_setup()
    _L0_conv_in = {k: v for k, v in _L0_conv_all.items() if k in ('qkv_w', 'qkv_b', 'pos_enc', 'proj_w', 'proj_b', )}
    del _L0_conv_all

    return {
        "x": x,
        "L0_conv_qkv_w": _L0_conv_in["qkv_w"],
        "L0_conv_qkv_b": _L0_conv_in["qkv_b"],
        "L0_conv_pos_enc": _L0_conv_in["pos_enc"],
        "L0_conv_proj_w": _L0_conv_in["proj_w"],
        "L0_conv_proj_b": _L0_conv_in["proj_b"],
    }

def reference(x, L0_conv_qkv_w, L0_conv_qkv_b, L0_conv_pos_enc, L0_conv_proj_w, L0_conv_proj_b):
    import jax
    import jax.numpy as jnp
    def _L0_conv_ref(x, qkv_w, qkv_b, pos_enc, proj_w, proj_b):
        import jax, jax.numpy as jnp
        import numpy as np
        NUM_HEADS = 8
        b1, c1, h1, w1 = x.shape
        h = NUM_HEADS
        xt = x.reshape(b1, c1, -1).transpose(0, 2, 1)
        B, N, C = xt.shape
        qkv = xt @ qkv_w.T + qkv_b
        q, k, v = jnp.split(qkv, 3, axis=-1)
        k = k + pos_enc[:, :N, :]
        q = jax.nn.relu(q)
        k = jax.nn.relu(k)

        def to_heads(t):
            return t.reshape(B, N, h, C // h).transpose(0, 2, 1, 3).reshape(B * h, N, C // h)
        q, k, v = map(to_heads, (q, k, v))
        i, j = (q.shape[-2], k.shape[-2])
        c, d = (k.shape[-1], v.shape[-1])
        q = q.astype(jnp.float32)
        k = k.astype(jnp.float32)
        v = v.astype(jnp.float32)
        z = 1.0 / (jnp.einsum('bic,bc->bi', q, k.sum(axis=1)) + 1e-06)
        if i * j * (c + d) > c * d * (i + j):
            kv = jnp.einsum('bjc,bjd->bcd', k, v)
            out = jnp.einsum('bic,bcd,bi->bid', q, kv, z)
        else:
            qk = jnp.einsum('bic,bjc->bij', q, k)
            out = jnp.einsum('bij,bjd,bi->bid', qk, v, z)
        out = out.reshape(B, h, N, C // h).transpose(0, 2, 1, 3).reshape(B, N, C)
        out = out @ proj_w.T + proj_b
        return out.transpose(0, 2, 1).reshape(b1, c1, h1, w1)

    def _gn(v, G=32, eps=1e-5):
        B_, C_, H_, W_ = v.shape
        g = v.reshape(B_, G, C_ // G, H_, W_)
        m = jnp.mean(g, axis=(2, 3, 4), keepdims=True)
        s = jnp.var(g, axis=(2, 3, 4), keepdims=True)
        return ((g - m) / jnp.sqrt(s + eps)).reshape(v.shape)

    def _ln_c(v, eps=1e-6):
        m = jnp.mean(v, axis=1, keepdims=True)
        s = jnp.var(v, axis=1, keepdims=True)
        return (v - m) / jnp.sqrt(s + eps)

    def _ln_t(v, eps=1e-5):
        m = jnp.mean(v, axis=-1, keepdims=True)
        s = jnp.var(v, axis=-1, keepdims=True)
        return (v - m) / jnp.sqrt(s + eps)

    def _to_tokens(v):
        B_, C_, H_, W_ = v.shape
        return v.reshape(B_, C_, H_ * W_).transpose(0, 2, 1)
    def _from_tokens(t, like):
        B_, C_, H_, W_ = like.shape
        return t.transpose(0, 2, 1).reshape(B_, C_, H_, W_)

    x = x + _L0_conv_ref(_gn(x), L0_conv_qkv_w, L0_conv_qkv_b, L0_conv_pos_enc, L0_conv_proj_w, L0_conv_proj_b)
    return x


_drawn_inputs = setup_inputs


def setup_inputs(seed=0):
    import zlib

    import numpy as np

    out = dict(_drawn_inputs(seed))
    spreads = {}
    factors = {'L0_conv_pos_enc': 8.0, 'L0_conv_proj_b': 2.705}
    for name, (base, spread) in spreads.items():
        noise = np.random.default_rng([zlib.crc32(name.encode()), seed]).standard_normal(out[name].shape)
        drawn = base * np.exp(spread * noise) if base else spread * noise
        out[name] = jnp.asarray(drawn.astype(out[name].dtype))
    for name, factor in factors.items():
        out[name] = (out[name] * factor).astype(out[name].dtype)
    return out
```

```python
from contextlib import ExitStack

import numpy as np

import concourse.bass as bass
from concourse import mybir

B, C, H, W = 16, 256, 80, 80
N = H * W
HEADS = 8
HD = C // HEADS
P = 128
CC = C // P
GROUP = C // 32
BLK = 512
HALF = BLK // 2
TILES = HALF // P
HEAD = N % BLK
NBLK = 1 + N // BLK
NHB = N // HALF
HPC = P // HD
SLOTS = 20
EARLY = SLOTS - NBLK
GRP0 = 7
WIN = 4 * (GRP0 - 1)
PRIME, PRIME_DMA = 1, 16
GN_EPS = 1e-5
Z_EPS = 1e-6


def build(nc, x, wqk_d, wv_d, pw_d, bq_d, bk_d, bv_d, pb_d, pos, ident_d, gavg_d, hmask_d, bmask_d, esel_d, posb_d, y):
    F32 = mybir.dt.float32
    F32R = mybir.dt.float32r
    ALU = mybir.AluOpType
    ACT = mybir.ActivationFunctionType
    ctx = ExitStack()
    with ctx:
        def sb(name, shape, dt=F32):
            return ctx.enter_context(nc.sbuf_tensor(name, shape, dt))

        def ps(name, shape):
            return ctx.enter_context(nc.psum_tensor(name, shape, F32))

        def sem(name):
            return ctx.enter_context(nc.semaphore(name))

        ring = sb("ring", [P, SLOTS, CC, BLK])
        q = sb("q", [P, CC, N])
        hl = sb("hl", [P, 2, 2, CC, BLK], F32R)
        xn = sb("xn", [P, 2, CC, HALF])
        xt = sb("xt", [P, 2, 2, TILES, C], F32R)
        kk = sb("kk", [P, 2, TILES, 2, C], F32R)
        kt = sb("kt", [P, TILES * C])
        posb = sb("posb", [P, 2, TILES * C])
        kacc = sb("kacc", [P, TILES, C])
        wqk = sb("wqk", [P, 2, CC, 2 * C], F32R)
        wv = sb("wv", [P, CC, C])
        pw = sb("pw", [P, CC, C])
        bpb = sb("bpb", [P, CC, C])
        esel = sb("esel", [P, GRP0 * CC, P], F32R)
        mhl = sb("mhl", [P, 2, CC, C], F32R)
        zhl = sb("zhl", [P, 2, BLK], F32R)
        swin = sb("swin", [P, CC, WIN + 64])
        zeros = sb("zeros", [P, P], F32R)
        ident = sb("ident", [P, P])
        gavg = sb("gavg", [P, P])
        bmask = sb("bmask", [P, P])
        hmask = sb("hmask", [P, HPC])
        ones = sb("ones", [P, 1])
        bq = sb("bq", [P, CC])
        bv = sb("bv", [P, CC])
        pb = sb("pb", [P, CC])
        ksc = sb("ksc", [P, CC])
        stats = sb("stats", [P, CC, NBLK, 6])
        mv = sb("mv", [P, CC, 2])
        landing = sb("landing", [P, 2])
        gmean = sb("gmean", [P, CC])
        gdev = sb("gdev", [P, CC])
        gvar = sb("gvar", [P, CC])
        gtmp = sb("gtmp", [P, CC])
        rstd = sb("rstd", [P, CC])

        psG = ps("psG", [P, CC, BLK])
        psT = ps("psT", [P, 2, BLK])
        psK = ps("psK", [P, 2, BLK])
        psQ = ps("psQ", [P, 2, BLK])

        w_loaded = sem("w_loaded")
        x_first = [sem(f"x_first{i}") for i in range(4)]
        pos_raw = [sem(f"pos_raw{i}") for i in range(2)]
        pos_added = sem("pos_added")
        pos_stored = [sem(f"pos_stored{i}") for i in range(2)]
        x_loaded = sem("x_loaded")
        pos_loaded = sem("pos_loaded")
        stored = sem("stored")
        w_high = sem("w_high")
        bvm_ready = sem("bvm_ready")
        bpb_done = sem("bpb_done")
        setup_done = sem("setup_done")
        stats_done = sem("stats_done")
        gn_step = sem("gn_step")
        gn_mean = sem("gn_mean")
        gn_var = sem("gn_var")
        gn_sqrt = sem("gn_sqrt")
        xn_ready = sem("xn_ready")
        xh_ready = sem("xh_ready")
        xl_ready = sem("xl_ready")
        t_done = sem("t_done")
        k_done = sem("k_done")
        g_done = sem("g_done")
        q_done = sem("q_done")
        xth_ready = sem("xth_ready")
        xtl_ready = sem("xtl_ready")
        kt_ready = sem("kt_ready")
        kr_ready = sem("kr_ready")
        kh_ready = sem("kh_ready")
        kl_ready = sem("kl_ready")
        kacc_zero = sem("kacc_zero")
        kacc_done = sem("kacc_done")
        q_saved = sem("q_saved")
        ksum_done = sem("ksum_done")
        ksc_ready = sem("ksc_ready")
        swin_ready = sem("swin_ready")
        gl_copied = sem("gl_copied")
        gt_ready = sem("gt_ready")
        kv_done = sem("kv_done")
        kvm_ready = sem("kvm_ready")
        m_done = sem("m_done")
        m_sum = sem("m_sum")
        mh_ready = sem("mh_ready")
        ml_ready = sem("ml_ready")
        den_done = sem("den_done")
        zt_step = sem("zt_step")
        zh_ready = sem("zh_ready")
        zl_ready = sem("zl_ready")
        zb_done = sem("zb_done")
        u_ready = sem("u_ready")
        uh_ready = sem("uh_ready")
        ul_ready = sem("ul_ready")
        o_done = sem("o_done")
        out_ready = sem("out_ready")

        wqk_raw = q[:, 0, 0:CC * 2 * C].rearrange("p (c n) -> p c n", c=CC)
        esel_raw = q[:, 0, 2048:2048 + GRP0 * CC * P].rearrange("p (j n) -> p j n", n=P)
        bvm = q[:, 1, 0:CC * P].rearrange("p (c n) -> p c n", c=CC)
        bk_b = ring[:, SLOTS - 1, 0, :]
        PIECES, PH = 5, NHB // 5
        piece = [ring[:, NBLK + 3 * i:NBLK + 3 * i + 3, :, :].rearrange("p s c n -> p (s c n)")[:, 0:PH * HALF * CC]
                 for i in range(2)]

        def start(t):
            return HEAD + (t - 1) * BLK

        def slot(b, t):
            return (NBLK * b + t) % SLOTS

        def cols(t, n):
            return bass.ds(0 if n == HEAD else start(t), n)

        block = ctx.enter_context(nc.Block())

        primed = [xtl_ready, kt_ready, out_ready, t_done, xh_ready, xl_ready, kacc_done, kl_ready, g_done, o_done]
        primed_dma = [x_loaded, stored]

        @block.sync
        def _(sp):
            smalls = [(wqk_raw, wqk_d.rearrange("c p n -> p c n")), (esel_raw, esel_d), (wv[:], wv_d.rearrange("c p n -> p c n")),
                      (pw[:], pw_d.rearrange("c p n -> p c n")), (ident[:], ident_d), (gavg[:], gavg_d),
                      (bmask[:], bmask_d), (hmask[:], hmask_d), (bq[:], bq_d), (bv[:], bv_d), (pb[:], pb_d)]

            def load_piece(k):
                if k >= 2:
                    sp.wait_ge(pos_stored[k % 2], 16 * (k // 2))
                src = pos[k * PH * HALF:(k + 1) * PH * HALF, :].rearrange("(g p) n -> p g n", p=P)
                sp.dma_start(piece[k % 2].rearrange("p (g n) -> p g n", n=C), src).then_inc(pos_raw[k % 2], 16)

            def store_piece(k):
                sp.wait_ge(pos_added, k + 1)
                dst = posb_d[k * PH:(k + 1) * PH].rearrange("h p n -> p h n")
                sp.dma_start(dst, piece[k % 2].rearrange("p (h n) -> p h n", n=TILES * C)).then_inc(pos_stored[k % 2], 16)

            for i in range(TILES):
                sp.dma_start(bk_b[:, i * C:(i + 1) * C], bk_d.partition_broadcast(P)).then_inc(w_loaded, 16)
            load_piece(0)
            load_piece(1)
            for dst, src in smalls:
                sp.dma_start(dst, src).then_inc(w_loaded, 16)

            def load_x(b, t, n):
                return sp.dma_start(ring[:, slot(b, t), :, 0:n],
                                    x[b, :, :, cols(t, n)].rearrange("c p n -> p c n"))

            for t in range(NBLK):
                if t >= 4:
                    sp.wait_ge(x_first[t % 4], 16 * (t // 4))
                load_x(0, t, HEAD if t == 0 else BLK).then_inc(x_first[t % 4], 16)
                if t % 3 == 2 and t < 12:
                    store_piece(t // 3)
                    if t // 3 + 2 < PIECES:
                        load_piece(t // 3 + 2)
            store_piece(PIECES - 1)
            sp.wait_ge(pos_stored[0], 16 * 3)
            sp.wait_ge(pos_stored[1], 16 * 2)

            def load_pos_at(b, h, parity):
                sp.wait_ge(kt_ready, PRIME + NHB * b + h - 1)
                sp.wait_ge(pos_loaded, (16 * NHB) * b + 16 * h)
                sp.dma_start(posb[:, parity, :], posb_d[h, :, :]).then_inc(pos_loaded, 16)

            def load_next_x(b, t, n):
                sp.wait_ge(x_loaded, PRIME_DMA + 16 * (NBLK * b + t))
                load_x(b + 1, t, n).then_inc(x_loaded, 16)

            def store_y(b, t, n):
                sp.wait_ge(out_ready, PRIME + CC * (NBLK * b + t + 1))
                sp.wait_ge(stored, PRIME_DMA + (16 * NBLK) * b + 16 * t)
                sp.dma_start(y[b, :, :, cols(t, n)].rearrange("c p n -> p c n"),
                             ring[:, slot(b, t), :, 0:n]).then_inc(stored, 16)

            def batch(b, last):
                def pos_pair(i):
                    load_pos_at(b, 2 * i + 2, 0)
                    load_pos_at(b, 2 * i + 3, 1)
                with sp.Fori(0, 5) as i:
                    pos_pair(i)
                if not last:
                    sp.wait_ge(stored, PRIME_DMA + 16 * NBLK * b)
                    load_next_x(b, 0, HEAD)
                with sp.Fori(0, EARLY - 1) as i:
                    load_pos_at(b, 2 * i + 12, 0)
                    load_pos_at(b, 2 * i + 13, 1)
                    if not last:
                        load_next_x(b, i + 1, BLK)
                load_pos_at(b, NHB - 1, 0)
                store_y(b, 0, HEAD)
                with sp.Fori(0, 3) as i:
                    for s in (1, 2):
                        store_y(b, 2 * i + s, BLK)
                        if not last:
                            load_next_x(b, 2 * i + s + EARLY - 1, BLK)
                if not last:
                    sp.wait_ge(ml_ready, b + 1)
                    for h in range(2):
                        sp.wait_ge(pos_loaded, 16 * (NHB * (b + 1) + h))
                        sp.dma_start(posb[:, h, :], posb_d[h, :, :]).then_inc(pos_loaded, 16)
                with sp.Fori(3, 6) as i:
                    for s in (1, 2):
                        store_y(b, 2 * i + s, BLK)

            for h in range(2):
                sp.dma_start(posb[:, h, :], posb_d[h, :, :]).then_inc(pos_loaded, 16)
                sp.wait_ge(pos_loaded, 16 * (h + 1))
            with sp.Fori(0, B - 1) as b:
                batch(b, False)
            batch(B - 1, True)
            sp.wait_ge(stored, PRIME_DMA + 16 * NBLK * B)

        @block.tensor
        def _(pe):
            mm = nc.tensor.matmul

            def gn_group_mean(b):
                pe.wait_ge(gn_step, 10 * b + 1)
                mm(psT[:, 0, 0:CC], gavg[:], mv[:, :, 0], start=True, stop=True).then_inc(gn_mean, 1)

            def gn_group_var(b):
                pe.wait_ge(gn_step, 10 * b + 4)
                mm(psT[:, 0, 0:CC], gavg[:], gvar[:], start=True, stop=True).then_inc(gn_var, 1)

            pe.wait_ge(bvm_ready, 1)
            for c in range(CC):
                last = mm(psK[:, 0, c * C:(c + 1) * C], bvm[:, c, :], pw[:, c, :], start=True, stop=True)
            last.then_inc(bpb_done, 1)
            gn_group_mean(0)
            gn_group_var(0)
            pe.wait_ge(setup_done, 1)

            def transpose_and_k(b, h, par, hp, tok):
                n = NHB * b + h
                pe.wait_ge(xh_ready, PRIME + n + 1)
                pe.wait_ge(xl_ready, PRIME + n + 1)
                if not (isinstance(h, int) and h == 0):
                    pe.wait_ge(xtl_ready, PRIME + n - 1)
                for i in range(TILES):
                    for c in range(CC):
                        last = nc.tensor.transpose(psT[:, hp, i * C + c * P:i * C + (c + 1) * P],
                                                   xn[:, hp, c, i * P:(i + 1) * P], ident[:])
                last.then_inc(t_done, 1)
                if not (isinstance(h, int) and h == 0):
                    pe.wait_ge(kt_ready, PRIME + n - 1)
                for i in range(TILES):
                    s = tok + i * P
                    terms = [(c, a, w) for c in range(CC) for a, w in ((0, 0), (0, 1), (1, 0))]
                    for j, (c, a, w) in enumerate(terms):
                        last = mm(psK[:, hp, i * C:(i + 1) * C], hl[:, par, a, c, s:s + P], wqk[:, w, c, C:2 * C],
                                  start=(j == 0), stop=(j == len(terms) - 1))
                last.then_inc(k_done, 1)

            def gram(b, h, hp, stop=False):
                n = NHB * b + h
                pe.wait_ge(xtl_ready, PRIME + n + 1)
                pe.wait_ge(kl_ready, PRIME + n + 1)
                for i in range(TILES):
                    for c in range(CC):
                        mm(psG[:, c, :], xt[:, hp, 0, i, c * P:(c + 1) * P], kk[:, hp, i, :, :],
                           start=False, stop=False)
                        last = mm(psG[:, c, C:2 * C], xt[:, hp, 1, i, c * P:(c + 1) * P], kk[:, hp, i, 0, :],
                                  start=False, stop=stop and i == TILES - 1)
                last.then_inc(g_done, 1)

            def query(b, t, par, n, m):
                if n == HEAD:
                    pe.wait_ge(out_ready, PRIME + CC * NBLK * b)
                else:
                    pe.wait_ge(q_saved, CC * (NBLK * b + t) + m - 1)
                terms = [(c, a, w) for c in range(CC) for w, a in ((0, 0), (0, 1), (1, 0))]
                for j, (c, a, w) in enumerate(terms):
                    last = mm(psQ[:, m, 0:n], wqk[:, w, c, m * P:(m + 1) * P], hl[:, par, a, c, 0:n],
                              start=(j == 0), stop=(j == len(terms) - 1))
                last.then_inc(q_done, 1)

            def denominators(b, g):
                blocks = list(range(GRP0)) if g == 0 else list(range(GRP0, NBLK))
                order = [t for t in blocks if t] + [t for t in blocks if not t]
                for a, t in enumerate(order):
                    n = BLK if t else HEAD
                    s = start(t) if t else 0
                    for c in range(CC):
                        w = WIN - 4 * (t - blocks[0])
                        last = mm(psT[0:64, g, 0:n], swin[:, c, w:w + 64], q[:, c, s:s + n],
                                  start=(a == 0 and c == 0), stop=(a == len(order) - 1 and c == CC - 1))
                last.then_inc(den_done, 1)

            def spread_z(b, t):
                n = BLK if t else HEAD
                g = 0 if t < GRP0 else 1
                if t in (0, GRP0):
                    pe.wait_ge(zl_ready, 2 * b + g + 1)
                if t:
                    pe.wait_ge(u_ready, NBLK * b + t)
                for c in range(CC):
                    last = mm(psG[:, c, 0:n], esel[:, (t - g * GRP0) * CC + c, :], zhl[:, g, 0:n],
                              start=True, stop=True)
                last.then_inc(zb_done, 1)

            def output(b, t):
                n = BLK if t else HEAD
                pe.wait_ge(uh_ready, NBLK * b + t + 1)
                pe.wait_ge(ul_ready, NBLK * b + t + 1)
                if t >= 2:
                    pe.wait_ge(out_ready, PRIME + CC * (NBLK * b + t - 1))
                psO = psK if t % 2 else psQ
                terms = [(c, a, w) for c in range(CC) for w, a in ((0, 0), (0, 1), (1, 0))]
                for m in range(CC):
                    for j, (c, a, w) in enumerate(terms):
                        last = mm(psO[:, m, 0:n], mhl[:, w, c, m * P:(m + 1) * P], hl[:, t % 2, a, c, 0:n],
                                  start=(j == 0), stop=(j == len(terms) - 1))
                last.then_inc(o_done, 1)

            def batch(b, last_batch):
                transpose_and_k(b, 0, 1, 0, 0)
                for c in range(CC):
                    mm(psG[:, c, :], zeros[:], esel[:, 0:4, :], start=True, stop=False)
                query(b, 0, 1, HEAD, 0)
                query(b, 0, 1, HEAD, 1)
                with pe.Fori(0, 6) as i:
                    for s in (1, 2):
                        t = 2 * i + s
                        par = (s + 1) % 2
                        transpose_and_k(b, 2 * t - 1, par, 1, 0)
                        gram(b, 2 * t - 2, 0)
                        pe.wait_ge(xl_ready, PRIME + NHB * b + 2 * t + 1)
                        query(b, t, par, BLK, 0)
                        transpose_and_k(b, 2 * t, par, 0, HALF)
                        gram(b, 2 * t - 1, 1)
                        query(b, t, par, BLK, 1)
                gram(b, NHB - 1, 0, stop=True)
                pe.wait_ge(kacc_done, PRIME + NHB * (b + 1))
                for c in range(CC):
                    for i in range(TILES):
                        last = mm(psK[:, 0, c:c + 1], kacc[:, i, c * P:(c + 1) * P], ones[:],
                                  start=(i == 0), stop=(i == TILES - 1))
                last.then_inc(ksum_done, 1)
                pe.wait_ge(gt_ready, b + 1)
                for c in range(CC):
                    for i in range(CC):
                        last = mm(psK[:, 1, c * P:(c + 1) * P], wv[:, i, c * P:(c + 1) * P],
                                  posb[:, 0, i * C + c * P:i * C + (c + 1) * P], start=(i == 0), stop=(i == CC - 1))
                last.then_inc(kv_done, 1)
                pe.wait_ge(swin_ready, b + 1)
                pe.wait_ge(q_saved, CC * NBLK * (b + 1))
                denominators(b, 0)
                pe.wait_ge(kvm_ready, b + 1)
                for c in range(CC):
                    last = mm(psQ[:, 0, c * C:(c + 1) * C], posb[:, 1, c * P:(c + 1) * P], pw[:, c, :],
                              start=True, stop=True)
                last.then_inc(m_done, 1)
                denominators(b, 1)
                spread_z(b, 0)
                pe.wait_ge(ml_ready, b + 1)
                for t in range(1, NBLK):
                    spread_z(b, t)
                    output(b, t - 1)
                    if not last_batch and t == NBLK - 2:
                        gn_group_mean(b + 1)
                    if not last_batch and t == NBLK - 1:
                        gn_group_var(b + 1)
                output(b, NBLK - 1)

            with pe.Fori(0, B - 1) as b:
                batch(b, False)
            batch(B - 1, True)

        @block.vector
        def _(dve):
            v = nc.vector

            def x_stats(b, t, n):
                for c in range(CC):
                    last = v.bn_stats(stats[:, c, t, :], ring[:, slot(b, t), c, 0:n])
                last.then_inc(stats_done, 1)

            def gn_channels(b):
                dve.wait_ge(stats_done, NBLK * (b + 1))
                v.tensor_copy(landing[:], stats[:, 0, 0, 0:2])
                for c in range(CC):
                    last = v.bn_aggr(mv[:, c, :], stats[:, c, :, :].rearrange("p t s -> p (t s)"))
                last.then_inc(gn_step, 1)

            def gn_offsets(b):
                dve.wait_ge(gn_mean, b + 1)
                dve.wait_ge(gn_step, 10 * b + 1)
                v.tensor_copy(gmean[:], psT[:, 0, 0:CC])
                v.tensor_tensor(gdev[:], mv[:, :, 0], psT[:, 0, 0:CC], ALU.subtract).then_inc(gn_step, 1)
                dve.wait_ge(gn_step, 10 * b + 2)
                v.tensor_tensor(gtmp[:], gdev[:], gdev[:], ALU.mult).then_inc(gn_step, 1)
                dve.wait_ge(gn_step, 10 * b + 3)
                v.tensor_tensor(gvar[:], gtmp[:], mv[:, :, 1], ALU.add).then_inc(gn_step, 1)

            def gn_rstd(b):
                dve.wait_ge(gn_var, b + 1)
                v.tensor_scalar(gvar[:], psT[:, 0, 0:CC], GN_EPS, None, ALU.add).then_inc(gn_step, 1)
                dve.wait_ge(gn_sqrt, b + 1)
                v.reciprocal(rstd[:], gtmp[:]).then_inc(gn_step, 1)
                dve.wait_ge(gn_step, 10 * b + 6)
                v.tensor_tensor(gdev[:], rstd[:], rstd[:], ALU.mult).then_inc(gn_step, 1)
                dve.wait_ge(gn_step, 10 * b + 7)
                v.tensor_tensor(gdev[:], gdev[:], gvar[:], ALU.mult).then_inc(gn_step, 1)
                dve.wait_ge(gn_step, 10 * b + 8)
                v.tensor_scalar(gdev[:], gdev[:], -0.5, 1.5, ALU.mult, ALU.add).then_inc(gn_step, 1)
                dve.wait_ge(gn_step, 10 * b + 9)
                v.tensor_tensor(rstd[:], rstd[:], gdev[:], ALU.mult).then_inc(gn_step, 1)
                dve.wait_ge(gn_step, 10 * b + 10)

            def normalise(b, t, h, hp, tok):
                n = NHB * b + h
                if isinstance(h, int) and h == 0:
                    if not (isinstance(b, int) and b == 0):
                        dve.wait_ge(t_done, PRIME + n)
                        dve.wait_ge(xh_ready, PRIME + n)
                        dve.wait_ge(xl_ready, PRIME + n)
                else:
                    dve.wait_ge(t_done, PRIME + n - 1)
                    dve.wait_ge(xh_ready, PRIME + n - 1)
                    dve.wait_ge(xl_ready, PRIME + n - 1)
                for c in range(CC):
                    last = v.tensor_scalar(xn[:, hp, c, :], ring[:, slot(b, t), c, tok:tok + HALF],
                                           gmean[:, c:c + 1], rstd[:, c:c + 1], ALU.subtract, ALU.mult)
                last.then_inc(xn_ready, 1)

            def key_rest(b, h, hp):
                n = NHB * b + h
                dve.wait_ge(k_done, n + 1)
                dve.wait_ge(pos_loaded, 16 * (n + 1))
                dve.wait_ge(kacc_done, PRIME + n)
                dve.wait_ge(kl_ready, PRIME + n)
                v.tensor_tensor(kt[:], psK[:, hp, :], posb[:, hp, :], ALU.add).then_inc(kt_ready, 1)
                dve.wait_ge(xth_ready, n + 1)
                v.tensor_tensor(xt[:, hp, 1, :, :].rearrange("p i n -> p (i n)"), psT[:, hp, :],
                                xt[:, hp, 0, :, :].rearrange("p i n -> p (i n)"), ALU.subtract).then_inc(xtl_ready, 1)
                dve.wait_ge(kh_ready, n + 1)
                v.tensor_tensor(kk[:, hp, :, 1, :], kt[:].rearrange("p (i n) -> p i n", i=TILES), kk[:, hp, :, 0, :],
                                ALU.subtract).then_inc(kl_ready, 1)

            def invert(b, g):
                dve.wait_ge(den_done, 2 * b + g + 1)
                v.tensor_scalar(kt[0:64, :], psT[0:64, g, :], Z_EPS, None, ALU.add).then_inc(zt_step, 1)
                dve.wait_ge(zt_step, 4 * b + 2 * g + 1)
                v.reciprocal(kt[0:64, :], kt[0:64, :]).then_inc(zt_step, 1)
                dve.wait_ge(zh_ready, 2 * b + g + 1)
                v.tensor_tensor(zhl[64:128, g, :], kt[0:64, :], zhl[0:64, g, :], ALU.subtract).then_inc(zl_ready, 1)

            def scale_q(b, t, n):
                dve.wait_ge(zb_done, NBLK * b + t + 1)
                v.tensor_tensor(q[:, :, cols(t, n)], q[:, :, cols(t, n)], psG[:, :, 0:n], ALU.mult).then_inc(u_ready, 1)

            def residual(b, t, n, psO):
                dve.wait_ge(o_done, PRIME + NBLK * b + t + 1)
                for m in range(CC):
                    xs = ring[:, slot(b, t), m, 0:n]
                    v.scalar_tensor_tensor(out=xs, in0=psO[:, m, 0:n], scalar=pb[:, m:m + 1], in1=xs,
                                           op0=ALU.add, op1=ALU.add).then_inc(out_ready, 1)

            v.memset(ones[:], 1.0)
            v.memset(kacc[:], 0.0).then_inc(kacc_zero, 1)
            v.memset(swin[:], 0.0)
            v.memset(zeros[:].bitcast(F32), 0.0)
            dve.wait_ge(w_loaded, 16 * 13)
            for c in range(CC):
                last = v.tensor_scalar(bvm[:, c, :], bmask[:], bv[:, c:c + 1], None, ALU.mult)
            last.then_inc(bvm_ready, 1)
            v.tensor_copy(esel[:], esel_raw)
            v.tensor_copy(wqk[:, 0, :, :], wqk_raw).then_inc(w_high, 1)
            dve.wait_ge(w_high, 1)
            v.tensor_tensor(wqk[:, 1, :, :], wqk_raw, wqk[:, 0, :, :], ALU.subtract)
            dve.wait_ge(bpb_done, 1)
            v.tensor_copy(bpb[:].rearrange("p c n -> p (c n)"), psK[:, 0, :]).then_inc(setup_done, 1)
            for k in range(PIECES):
                dve.wait_ge(pos_raw[k % 2], 16 * (k // 2 + 1))
                for h in range(PH):
                    seg = piece[k % 2][:, h * TILES * C:(h + 1) * TILES * C]
                    last = v.tensor_tensor(seg, seg, bk_b, ALU.add)
                last.then_inc(pos_added, 1)
            for t in range(NBLK):
                dve.wait_ge(x_first[t % 4], 16 * (t // 4 + 1))
                x_stats(0, t, BLK if t else HEAD)
            gn_channels(0)
            gn_offsets(0)
            gn_rstd(0)
            normalise(0, 0, 0, 0, 0)

            def batch(b, last_batch):
                def pair(i, with_stats):
                    for s in (1, 2):
                        t = 2 * i + s
                        normalise(b, t, 2 * t - 1, 1, 0)
                        key_rest(b, 2 * t - 2, 0)
                        normalise(b, t, 2 * t, 0, HALF)
                        key_rest(b, 2 * t - 1, 1)
                        if with_stats:
                            dve.wait_ge(x_loaded, PRIME_DMA + 16 * (NBLK * b + t - 5))
                            x_stats(b + 1, t - 6, BLK)
                with dve.Fori(0, 3) as i:
                    pair(i, False)
                if not last_batch:
                    dve.wait_ge(x_loaded, PRIME_DMA + 16 * (NBLK * b + 1))
                    x_stats(b + 1, 0, HEAD)
                with dve.Fori(3, 6) as i:
                    pair(i, not last_batch)
                key_rest(b, NHB - 1, 0)
                dve.wait_ge(ksum_done, b + 1)
                v.tensor_copy(ksc[:], psK[:, 0, 0:CC]).then_inc(ksc_ready, 1)
                v.memset(kacc[:], 0.0).then_inc(kacc_zero, 1)
                dve.wait_ge(ksc_ready, b + 1)
                for c in range(CC):
                    s = WIN + 32 * c
                    last = v.tensor_scalar(swin[:, c, s:s + HPC], hmask[:], ksc[:, c:c + 1], None, ALU.mult)
                last.then_inc(swin_ready, 1)
                gt = posb[:, 0, :].rearrange("p (c n) -> p c n", c=CC)
                dve.wait_ge(gl_copied, b + 1)
                v.tensor_tensor(gt, psG[:, :, 0:C], gt, ALU.add).then_inc(gt_ready, 1)
                dve.wait_ge(kv_done, b + 1)
                for c in range(CC):
                    last = v.tensor_tensor(posb[:, 1, c * P:(c + 1) * P], psK[:, 1, c * P:(c + 1) * P], bmask[:], ALU.mult)
                last.then_inc(kvm_ready, 1)
                dve.wait_ge(m_done, b + 1)
                for c in range(CC):
                    last = v.scalar_tensor_tensor(out=posb[:, 0, c * C:(c + 1) * C], in0=bpb[:, c, :], scalar=ksc[:, c:c + 1],
                                                  in1=psQ[:, 0, c * C:(c + 1) * C], op0=ALU.mult, op1=ALU.add)
                last.then_inc(m_sum, 1)
                dve.wait_ge(mh_ready, b + 1)
                v.tensor_tensor(mhl[:, 1, :, :].rearrange("p c n -> p (c n)"), posb[:, 0, :],
                                mhl[:, 0, :, :].rearrange("p c n -> p (c n)"), ALU.subtract).then_inc(ml_ready, 1)
                invert(b, 0)
                scale_q(b, 0, HEAD)

                def pair_b(i, first, with_stats):
                    for s in (1, 2):
                        t = 2 * i + s
                        scale_q(b, t, BLK)
                        residual(b, t - 1, HEAD if first and s == 1 else BLK, psQ if s == 1 else psK)
                        if with_stats and not last_batch:
                            dve.wait_ge(x_loaded, PRIME_DMA + 16 * (NBLK * b + t + 3))
                            x_stats(b + 1, t + 2, BLK)
                pair_b(0, True, False)
                invert(b, 1)
                pair_b(1, False, False)
                with dve.Fori(2, 5) as i:
                    pair_b(i, False, True)
                if last_batch:
                    pair_b(5, False, False)
                else:
                    gn_channels(b + 1)
                    scale_q(b, NBLK - 2, BLK)
                    residual(b, NBLK - 3, BLK, psQ)
                    gn_offsets(b + 1)
                    scale_q(b, NBLK - 1, BLK)
                    residual(b, NBLK - 2, BLK, psK)
                    gn_rstd(b + 1)
                    normalise(b + 1, 0, 0, 0, 0)
                residual(b, NBLK - 1, BLK, psQ)

            with dve.Fori(0, B - 1) as b:
                batch(b, False)
            batch(B - 1, True)

        @block.scalar
        def _(act):
            a = nc.scalar.activation

            def gn_root(b):
                act.wait_ge(gn_step, 10 * b + 5)
                a(gtmp[:], gvar[:], ACT.Sqrt).then_inc(gn_sqrt, 1)

            def xn_high(b, h, par, hp, tok, free):
                act.wait_ge(xn_ready, NHB * b + h + 1)
                free(act)
                a(hl[:, par, 0, :, tok:tok + HALF], xn[:, hp, :, :], ACT.Copy).then_inc(xh_ready, 1)

            def rest(b, h, hp):
                n = NHB * b + h
                act.wait_ge(t_done, PRIME + n + 1)
                if isinstance(h, int) and h == 0:
                    act.wait_ge(g_done, PRIME + n)
                else:
                    act.wait_ge(g_done, PRIME + n - 1)
                a(xt[:, hp, 0, :, :].rearrange("p i n -> p (i n)"), psT[:, hp, :], ACT.Copy).then_inc(xth_ready, 1)
                act.wait_ge(kt_ready, PRIME + n + 1)
                a(kt[:], kt[:], ACT.Relu).then_inc(kr_ready, 1)
                act.wait_ge(kr_ready, n + 1)
                a(kk[:, hp, :, 0, :], kt[:].rearrange("p (i n) -> p i n", i=TILES), ACT.Copy).then_inc(kh_ready, 1)

            def save_q(b, t, n, m):
                act.wait_ge(q_done, CC * (NBLK * b + t) + m + 1)
                a(q[:, m, cols(t, n)], psQ[:, m, 0:n], ACT.Relu, bias=bq[:, m:m + 1]).then_inc(q_saved, 1)

            def block_free(b, t):
                return lambda eng: eng.wait_ge(q_done, CC * (NBLK * b + t - 1))

            def phase_free(b, k):
                return lambda eng: eng.wait_ge(o_done, PRIME + NBLK * b + k)

            def z_high(b, g):
                act.wait_ge(zt_step, 4 * b + 2 * g + 2)
                a(zhl[0:64, g, :], kt[0:64, :], ACT.Copy).then_inc(zh_ready, 1)

            def u_high(b, t, n, par):
                act.wait_ge(u_ready, NBLK * b + t + 1)
                if not (isinstance(t, int) and t < 2):
                    act.wait_ge(o_done, PRIME + NBLK * b + t - 1)
                a(hl[:, par, 0, :, 0:n], q[:, :, cols(t, n)], ACT.Copy).then_inc(uh_ready, 1)

            gn_root(0)
            xn_high(0, 0, 1, 0, 0, lambda eng: None)

            def batch(b, last_batch):
                xn_high(b, 1, 0, 1, 0, phase_free(b, 0))
                rest(b, 0, 0)
                save_q(b, 0, HEAD, 0)
                save_q(b, 0, HEAD, 1)
                xn_high(b, 2, 0, 0, HALF, phase_free(b, 0))
                rest(b, 1, 1)
                save_q(b, 1, BLK, 0)

                def step(t, par):
                    xn_high(b, 2 * t - 1, par, 1, 0, block_free(b, t))
                    save_q(b, t - 1, BLK, 1)
                    rest(b, 2 * t - 2, 0)
                    xn_high(b, 2 * t, par, 0, HALF, block_free(b, t))
                    rest(b, 2 * t - 1, 1)
                    save_q(b, t, BLK, 0)
                with act.Fori(0, 5) as i:
                    step(2 * i + 2, 1)
                    step(2 * i + 3, 0)
                step(NBLK - 1, 1)
                save_q(b, NBLK - 1, BLK, 1)
                rest(b, NHB - 1, 0)
                act.wait_ge(g_done, PRIME + NHB * (b + 1))
                act.wait_ge(kt_ready, PRIME + NHB * (b + 1))
                a(posb[:, 0, :].rearrange("p (c n) -> p c n", c=CC), psG[:, :, C:2 * C], ACT.Copy).then_inc(gl_copied, 1)
                act.wait_ge(m_sum, b + 1)
                a(mhl[:, 0, :, :].rearrange("p c n -> p (c n)"), posb[:, 0, :], ACT.Copy).then_inc(mh_ready, 1)
                z_high(b, 0)
                u_high(b, 0, HEAD, 0)
                u_high(b, 1, BLK, 1)
                u_high(b, 2, BLK, 0)
                z_high(b, 1)
                with act.Fori(1, 6) as i:
                    u_high(b, 2 * i + 1, BLK, 1)
                    u_high(b, 2 * i + 2, BLK, 0)
                if not last_batch:
                    gn_root(b + 1)
                    xn_high(b + 1, 0, 1, 0, 0, phase_free(b, NBLK - 1))

            with act.Fori(0, B - 1) as b:
                batch(b, False)
            batch(B - 1, True)

        @block.gpsimd
        def _(pool):
            g = nc.gpsimd

            def xn_low(b, h, par, hp, tok):
                pool.wait_ge(xh_ready, PRIME + NHB * b + h + 1)
                g.tensor_tensor(hl[:, par, 1, :, tok:tok + HALF], xn[:, hp, :, :], hl[:, par, 0, :, tok:tok + HALF],
                                ALU.subtract).then_inc(xl_ready, 1)

            def key_sum(b, h):
                n = NHB * b + h
                pool.wait_ge(kr_ready, n + 1)
                pool.wait_ge(kacc_zero, b + 1)
                pool.wait_ge(kacc_done, PRIME + n)
                g.tensor_tensor(kacc[:].rearrange("p i n -> p (i n)"), kacc[:].rearrange("p i n -> p (i n)"), kt[:],
                                ALU.add).then_inc(kacc_done, 1)

            def u_low(b, t, n, par):
                pool.wait_ge(uh_ready, NBLK * b + t + 1)
                g.tensor_tensor(hl[:, par, 1, :, 0:n], q[:, :, cols(t, n)], hl[:, par, 0, :, 0:n],
                                ALU.subtract).then_inc(ul_ready, 1)

            for s in primed:
                pool.sem_inc(s, PRIME)
            for s in primed_dma:
                pool.sem_inc(s, PRIME_DMA)
            xn_low(0, 0, 1, 0, 0)

            def batch(b, last_batch):
                with pool.Fori(0, 6) as i:
                    for s in (1, 2):
                        t = 2 * i + s
                        par = (s + 1) % 2
                        xn_low(b, 2 * t - 1, par, 1, 0)
                        key_sum(b, 2 * t - 2)
                        xn_low(b, 2 * t, par, 0, HALF)
                        key_sum(b, 2 * t - 1)
                key_sum(b, NHB - 1)
                u_low(b, 0, HEAD, 0)
                with pool.Fori(0, 6) as i:
                    u_low(b, 2 * i + 1, BLK, 1)
                    u_low(b, 2 * i + 2, BLK, 0)
                if not last_batch:
                    xn_low(b + 1, 0, 1, 0, 0)

            with pool.Fori(0, B - 1) as b:
                batch(b, False)
            batch(B - 1, True)


def kernel(**inputs):
    import concourse.bacc as bacc
    from concourse.bass_utils import run_bass_kernel_spmd

    x = np.ascontiguousarray(inputs["x"])
    qkv_w = np.asarray(inputs["L0_conv_qkv_w"])
    qkv_b = np.asarray(inputs["L0_conv_qkv_b"])
    proj_w = np.asarray(inputs["L0_conv_proj_w"])
    proj_b = np.asarray(inputs["L0_conv_proj_b"])
    chan = np.arange(P)
    same_head = (chan[:, None] // HD == chan[None, :] // HD)
    row = 32 * np.arange(CC)[None, :, None] + 4 * np.arange(GRP0)[:, None, None] + (chan // HD)[None, None, :]
    esel = (np.arange(P)[:, None, None, None] % 64 == row[None]).reshape(P, GRP0 * CC, P)
    arrays = {
        "x": x.reshape(B, CC, P, N),
        "wqk": np.ascontiguousarray(qkv_w[:2 * C].T).reshape(CC, P, 2 * C),
        "wv": np.ascontiguousarray(qkv_w[2 * C:].T).reshape(CC, P, C),
        "pw": np.ascontiguousarray(proj_w.T).reshape(CC, P, C),
        "bq": np.ascontiguousarray(qkv_b[:C].reshape(CC, P).T),
        "bk": np.ascontiguousarray(qkv_b[C:2 * C].reshape(1, C)),
        "bv": np.ascontiguousarray(qkv_b[2 * C:].reshape(CC, P).T),
        "pb": np.ascontiguousarray(proj_b.reshape(CC, P).T),
        "pos": np.ascontiguousarray(np.asarray(inputs["L0_conv_pos_enc"]).reshape(N, C)),
        "ident": np.eye(P, dtype=np.float32),
        "gavg": (chan[:, None] // GROUP == chan[None, :] // GROUP).astype(np.float32) / GROUP,
        "hmask": (chan[:, None] // HD == np.arange(HPC)[None, :]).astype(np.float32),
        "bmask": same_head.astype(np.float32),
        "esel": esel.astype(np.float32),
    }
    arrays = {f"in_{name}": a for name, a in arrays.items()}
    nc = bacc.Bacc("TRN2", target_bir_lowering=False, num_devices=1)
    f32 = mybir.dt.float32
    args = [nc.dram_tensor(name, a.shape, f32, kind="ExternalInput").ap() for name, a in arrays.items()]
    posb = nc.dram_tensor("pos_plus_bk", (NHB, P, TILES * C), f32, kind="Internal").ap()
    y = nc.dram_tensor("y", (B, CC, P, N), f32, kind="ExternalOutput").ap()
    build(nc, *args, posb, y)
    r = run_bass_kernel_spmd(nc, [arrays], core_ids=[0])
    return r.results[0]["y"].reshape(B, C, H, W)
```

```python
from contextlib import ExitStack

import numpy as np

import concourse.bass as bass
from concourse import mybir

B, C, H, W = 16, 256, 80, 80
N = H * W
HEADS = 8
HD = C // HEADS
P = 128
CC = C // P
GROUP = C // 32
BLK = 512
HALF = BLK // 2
TILES = HALF // P
HEAD = N % BLK
NBLK = 1 + N // BLK
NHB = N // HALF
HPC = P // HD
SLOTS = 22
EARLY = SLOTS - NBLK
GRP0 = 7
WIN = 4 * (GRP0 - 1)
STATS_AT = (5, 6, 7, 8)
PRIME, PRIME_DMA = 3, 16
GN_EPS = 1e-5
Z_EPS = 1e-6


def build(nc, x, wqk_d, wv_d, pw_d, bq_d, bk_d, bv_d, pb_d, pos, ident_d, gavg_d, hmask_d, bmask_d, esel_d, posb_d, y):
    F32 = mybir.dt.float32
    F32R = mybir.dt.float32r
    ALU = mybir.AluOpType
    ACT = mybir.ActivationFunctionType
    ctx = ExitStack()
    with ctx:
        def sb(name, shape, dt=F32):
            return ctx.enter_context(nc.sbuf_tensor(name, shape, dt))

        def ps(name, shape):
            return ctx.enter_context(nc.psum_tensor(name, shape, F32))

        def sem(name):
            return ctx.enter_context(nc.semaphore(name))

        ring = sb("ring", [P, SLOTS, CC, BLK])
        q = sb("q", [P, CC, N])
        hl = sb("hl", [P, 2, 2, CC, BLK], F32R)
        xn = sb("xn", [P, 2, CC, HALF])
        xt = sb("xt", [P, 2, 2, TILES, C], F32R)
        kk = sb("kk", [P, 2, TILES, 2, C], F32R)
        kt = sb("kt", [P, TILES * C])
        posb = sb("posb", [P, 2, TILES * C])
        kacc = sb("kacc", [P, TILES, C])
        wqk = sb("wqk", [P, 2, CC, 2 * C], F32R)
        wv = sb("wv", [P, CC, C])
        pw = sb("pw", [P, CC, C])
        bpb = sb("bpb", [P, CC, C])
        esel = sb("esel", [P, GRP0 * CC, P], F32R)
        xtu = xt[:].rearrange("p a l i n -> p (a l) (i n)").rearrange("p (l c) n -> p l c n", l=2)
        ubuf = [hl[:, 0], hl[:, 1], xtu]
        mhl = kk[:, 0, :, :, :]
        zhl = kk[:, 1, :, :, :].rearrange("p i a n -> p i (a n)")
        swin = sb("swin", [P, CC, WIN + 64])
        zeros = sb("zeros", [P, P], F32R)
        ident = sb("ident", [P, P])
        gavg = sb("gavg", [P, P])
        bmask = sb("bmask", [P, P])
        hmask = sb("hmask", [P, HPC])
        ones = sb("ones", [P, 1])
        bq = sb("bq", [P, CC])
        bv = sb("bv", [P, CC])
        pb = sb("pb", [P, CC])
        ksc = sb("ksc", [P, CC])
        stats = sb("stats", [P, CC, NBLK, 6])
        mv = sb("mv", [P, CC, 2])
        landing = sb("landing", [P, 2])
        gmean = sb("gmean", [P, CC])
        gdev = sb("gdev", [P, CC])
        gvar = sb("gvar", [P, CC])
        gtmp = sb("gtmp", [P, CC])
        rstd = sb("rstd", [P, CC])

        psG = ps("psG", [P, CC, BLK])
        psT = ps("psT", [P, 2, BLK])
        psK = ps("psK", [P, 2, BLK])
        psQ = ps("psQ", [P, 2, BLK])

        w_loaded = sem("w_loaded")
        x_first = [sem(f"x_first{i}") for i in range(4)]
        pos_raw = [sem(f"pos_raw{i}") for i in range(2)]
        pos_added = sem("pos_added")
        pos_stored = [sem(f"pos_stored{i}") for i in range(2)]
        x_loaded = sem("x_loaded")
        pos_loaded = sem("pos_loaded")
        stored = sem("stored")
        w_high = sem("w_high")
        bvm_ready = sem("bvm_ready")
        bpb_done = sem("bpb_done")
        setup_done = sem("setup_done")
        stats_done = sem("stats_done")
        gn_step = sem("gn_step")
        gn_mean = sem("gn_mean")
        gn_var = sem("gn_var")
        gn_sqrt = sem("gn_sqrt")
        xn_ready = sem("xn_ready")
        xh_ready = sem("xh_ready")
        xl_ready = sem("xl_ready")
        t_done = sem("t_done")
        k_done = sem("k_done")
        g_done = sem("g_done")
        q_done = sem("q_done")
        xth_ready = sem("xth_ready")
        xtl_ready = sem("xtl_ready")
        kt_ready = sem("kt_ready")
        kr_ready = sem("kr_ready")
        kh_ready = sem("kh_ready")
        kl_ready = sem("kl_ready")
        kacc_zero = sem("kacc_zero")
        kacc_done = sem("kacc_done")
        q_saved = sem("q_saved")
        ksum_done = sem("ksum_done")
        ksc_ready = sem("ksc_ready")
        swin_ready = sem("swin_ready")
        gl_copied = sem("gl_copied")
        gt_ready = sem("gt_ready")
        kv_done = sem("kv_done")
        kvm_ready = sem("kvm_ready")
        m_done = sem("m_done")
        m_sum = sem("m_sum")
        mh_ready = sem("mh_ready")
        ml_ready = sem("ml_ready")
        den_done = sem("den_done")
        zt_step = sem("zt_step")
        zh_ready = sem("zh_ready")
        zl_ready = sem("zl_ready")
        zb_done = sem("zb_done")
        u_ready = sem("u_ready")
        uh_ready = sem("uh_ready")
        ul_ready = sem("ul_ready")
        o_done = sem("o_done")
        out_ready = sem("out_ready")

        wqk_raw = q[:, 0, 0:CC * 2 * C].rearrange("p (c n) -> p c n", c=CC)
        esel_raw = q[:, 0, 2048:2048 + GRP0 * CC * P].rearrange("p (j n) -> p j n", n=P)
        bvm = q[:, 1, 0:CC * P].rearrange("p (c n) -> p c n", c=CC)
        bk_b = ring[:, SLOTS - 1, 0, :]
        PIECES, PH = 5, NHB // 5
        piece = [ring[:, NBLK + 3 * i:NBLK + 3 * i + 3, :, :].rearrange("p s c n -> p (s c n)")[:, 0:PH * HALF * CC]
                 for i in range(2)]

        def start(t):
            return HEAD + (t - 1) * BLK

        def slot(b, t):
            return (NBLK * b + t) % SLOTS

        def cols(t, n):
            return bass.ds(0 if n == HEAD else start(t), n)

        block = ctx.enter_context(nc.Block())

        primed = [xtl_ready, kt_ready, out_ready, t_done, xh_ready, xl_ready, kacc_done, kl_ready, g_done, o_done]
        primed_dma = [x_loaded, stored]

        @block.sync
        def _(sp):
            smalls = [(wqk_raw, wqk_d.rearrange("c p n -> p c n")), (esel_raw, esel_d), (wv[:], wv_d.rearrange("c p n -> p c n")),
                      (pw[:], pw_d.rearrange("c p n -> p c n")), (ident[:], ident_d), (gavg[:], gavg_d),
                      (bmask[:], bmask_d), (hmask[:], hmask_d), (bq[:], bq_d), (bv[:], bv_d), (pb[:], pb_d)]

            def load_piece(k):
                if k >= 2:
                    sp.wait_ge(pos_stored[k % 2], 16 * (k // 2))
                src = pos[k * PH * HALF:(k + 1) * PH * HALF, :].rearrange("(g p) n -> p g n", p=P)
                sp.dma_start(piece[k % 2].rearrange("p (g n) -> p g n", n=C), src).then_inc(pos_raw[k % 2], 16)

            def store_piece(k):
                sp.wait_ge(pos_added, k + 1)
                dst = posb_d[k * PH:(k + 1) * PH].rearrange("h p n -> p h n")
                sp.dma_start(dst, piece[k % 2].rearrange("p (h n) -> p h n", n=TILES * C)).then_inc(pos_stored[k % 2], 16)

            for i in range(TILES):
                sp.dma_start(bk_b[:, i * C:(i + 1) * C], bk_d.partition_broadcast(P)).then_inc(w_loaded, 16)
            load_piece(0)
            load_piece(1)
            for dst, src in smalls:
                sp.dma_start(dst, src).then_inc(w_loaded, 16)

            def load_x(b, t, n):
                return sp.dma_start(ring[:, slot(b, t), :, 0:n],
                                    x[b, :, :, cols(t, n)].rearrange("c p n -> p c n"))

            for t in range(NBLK):
                if t >= 4:
                    sp.wait_ge(x_first[t % 4], 16 * (t // 4))
                load_x(0, t, HEAD if t == 0 else BLK).then_inc(x_first[t % 4], 16)
                if t % 3 == 2 and t < 12:
                    store_piece(t // 3)
                    if t // 3 + 2 < PIECES:
                        load_piece(t // 3 + 2)
            store_piece(PIECES - 1)
            sp.wait_ge(pos_stored[0], 16 * 3)
            sp.wait_ge(pos_stored[1], 16 * 2)

            def load_pos_at(b, h, parity):
                sp.wait_ge(kt_ready, PRIME + NHB * b + h - 1)
                sp.wait_ge(pos_loaded, (16 * NHB) * b + 16 * h)
                sp.dma_start(posb[:, parity, :], posb_d[h, :, :]).then_inc(pos_loaded, 16)

            def load_next_x(b, t, n):
                sp.wait_ge(x_loaded, PRIME_DMA + 16 * (NBLK * b + t))
                load_x(b + 1, t, n).then_inc(x_loaded, 16)

            def store_y(b, t, n):
                sp.wait_ge(out_ready, PRIME + CC * (NBLK * b + t + 1))
                sp.wait_ge(stored, PRIME_DMA + (16 * NBLK) * b + 16 * t)
                sp.dma_start(y[b, :, :, cols(t, n)].rearrange("c p n -> p c n"),
                             ring[:, slot(b, t), :, 0:n]).then_inc(stored, 16)

            def batch(b, last):
                def pos_pair(i):
                    load_pos_at(b, 2 * i + 2, 0)
                    load_pos_at(b, 2 * i + 3, 1)
                with sp.Fori(0, NBLK - 1 - EARLY) as i:
                    pos_pair(i)
                if not last:
                    sp.wait_ge(stored, PRIME_DMA + 16 * NBLK * b)
                    load_next_x(b, 0, HEAD)
                with sp.Fori(0, EARLY - 1) as i:
                    load_pos_at(b, 2 * i + NHB - 1 - 2 * (EARLY - 1), 0)
                    load_pos_at(b, 2 * i + NHB - 2 * (EARLY - 1), 1)
                    if not last:
                        load_next_x(b, i + 1, BLK)
                load_pos_at(b, NHB - 1, 0)
                store_y(b, 0, HEAD)
                with sp.Fori(0, (NBLK - EARLY) // 2) as i:
                    for s in (1, 2):
                        store_y(b, 2 * i + s, BLK)
                        if not last:
                            load_next_x(b, 2 * i + s + EARLY - 1, BLK)
                if not last:
                    sp.wait_ge(ml_ready, b + 1)
                    for h in range(2):
                        sp.wait_ge(pos_loaded, 16 * (NHB * (b + 1) + h))
                        sp.dma_start(posb[:, h, :], posb_d[h, :, :]).then_inc(pos_loaded, 16)
                with sp.Fori((NBLK - EARLY) // 2, 6) as i:
                    for s in (1, 2):
                        store_y(b, 2 * i + s, BLK)

            for h in range(2):
                sp.dma_start(posb[:, h, :], posb_d[h, :, :]).then_inc(pos_loaded, 16)
                sp.wait_ge(pos_loaded, 16 * (h + 1))
            with sp.Fori(0, B - 1) as b:
                batch(b, False)
            batch(B - 1, True)
            sp.wait_ge(stored, PRIME_DMA + 16 * NBLK * B)

        @block.tensor
        def _(pe):
            mm = nc.tensor.matmul

            def gn_group_mean(b):
                pe.wait_ge(gn_step, 10 * b + 1)
                mm(psT[:, 0, 0:CC], gavg[:], mv[:, :, 0], start=True, stop=True).then_inc(gn_mean, 1)

            def gn_group_var(b):
                pe.wait_ge(gn_step, 10 * b + 4)
                mm(psT[:, 0, 0:CC], gavg[:], gvar[:], start=True, stop=True).then_inc(gn_var, 1)

            pe.wait_ge(bvm_ready, 1)
            for c in range(CC):
                last = mm(psK[:, 0, c * C:(c + 1) * C], bvm[:, c, :], pw[:, c, :], start=True, stop=True)
            last.then_inc(bpb_done, 1)
            gn_group_mean(0)
            gn_group_var(0)
            pe.wait_ge(setup_done, 1)

            def transpose_and_k(b, h, par, hp, tok):
                n = NHB * b + h
                pe.wait_ge(xh_ready, PRIME + n + 1)
                pe.wait_ge(xl_ready, PRIME + n + 1)
                if not (isinstance(h, int) and h == 0):
                    pe.wait_ge(xtl_ready, PRIME + n - 1)
                for i in range(TILES):
                    for c in range(CC):
                        last = nc.tensor.transpose(psT[:, hp, i * C + c * P:i * C + (c + 1) * P],
                                                   xn[:, hp, c, i * P:(i + 1) * P], ident[:])
                last.then_inc(t_done, 1)
                if isinstance(h, int) and h == 0:
                    pe.wait_ge(out_ready, PRIME + CC * (NBLK * b - 1))
                else:
                    pe.wait_ge(kt_ready, PRIME + n - 1)
                for i in range(TILES):
                    s = tok + i * P
                    terms = [(c, a, w) for c in range(CC) for a, w in ((0, 0), (0, 1), (1, 0))]
                    for j, (c, a, w) in enumerate(terms):
                        last = mm(psK[:, hp, i * C:(i + 1) * C], hl[:, par, a, c, s:s + P], wqk[:, w, c, C:2 * C],
                                  start=(j == 0), stop=(j == len(terms) - 1))
                last.then_inc(k_done, 1)

            def gram(b, h, hp, stop=False):
                n = NHB * b + h
                pe.wait_ge(xtl_ready, PRIME + n + 1)
                pe.wait_ge(kl_ready, PRIME + n + 1)
                for i in range(TILES):
                    for c in range(CC):
                        mm(psG[:, c, :], xt[:, hp, 0, i, c * P:(c + 1) * P], kk[:, hp, i, :, :],
                           start=False, stop=False)
                        last = mm(psG[:, c, C:2 * C], xt[:, hp, 1, i, c * P:(c + 1) * P], kk[:, hp, i, 0, :],
                                  start=False, stop=stop and i == TILES - 1)
                last.then_inc(g_done, 1)

            def query(b, t, par, n, m):
                if n == HEAD:
                    pe.wait_ge(out_ready, PRIME + CC * NBLK * b)
                else:
                    pe.wait_ge(q_saved, CC * (NBLK * b + t) + m - 1)
                terms = [(c, a, w) for c in range(CC) for w, a in ((0, 0), (0, 1), (1, 0))]
                for j, (c, a, w) in enumerate(terms):
                    last = mm(psQ[:, m, 0:n], wqk[:, w, c, m * P:(m + 1) * P], hl[:, par, a, c, 0:n],
                              start=(j == 0), stop=(j == len(terms) - 1))
                last.then_inc(q_done, 1)

            def denominators(g, lo, hi):
                blocks = list(range(GRP0)) if g == 0 else list(range(GRP0, NBLK))
                order = [t for t in blocks if t] + [t for t in blocks if not t]
                for a, t in list(enumerate(order))[lo:hi]:
                    n = BLK if t else HEAD
                    s = start(t) if t else 0
                    for c in range(CC):
                        w = WIN - 4 * (t - blocks[0])
                        last = mm(psT[0:64, g, 0:n], swin[:, c, w:w + 64], q[:, c, s:s + n],
                                  start=(a == 0 and c == 0), stop=(a == len(order) - 1 and c == CC - 1))
                if hi == len(order):
                    last.then_inc(den_done, 1)

            def spread_z(b, t):
                n = BLK if t else HEAD
                g = 0 if t < GRP0 else 1
                if t in (0, GRP0):
                    pe.wait_ge(zl_ready, 2 * b + g + 1)
                if t:
                    pe.wait_ge(u_ready, NBLK * b + t)
                for c in range(CC):
                    last = mm(psG[:, c, 0:n], esel[:, (t - g * GRP0) * CC + c, :], zhl[:, g, 0:n],
                              start=True, stop=True)
                last.then_inc(zb_done, 1)

            def output(b, t):
                n = BLK if t else HEAD
                psO = psK if t % 2 else psQ
                pe.wait_ge(uh_ready, NBLK * b + t + 1)
                if t >= 2:
                    pe.wait_ge(out_ready, PRIME + CC * (NBLK * b + t - 1))
                for m in range(CC):
                    for j, (c, w) in enumerate([(c, w) for c in range(CC) for w in range(2)]):
                        mm(psO[:, m, 0:n], mhl[:, w, c, m * P:(m + 1) * P], ubuf[t % 3][:, 0, c, 0:n],
                           start=(j == 0), stop=False)
                pe.wait_ge(ul_ready, NBLK * b + t + 1)
                for m in range(CC):
                    for c in range(CC):
                        last = mm(psO[:, m, 0:n], mhl[:, 0, c, m * P:(m + 1) * P], ubuf[t % 3][:, 1, c, 0:n],
                                  start=False, stop=(c == CC - 1))
                    last.then_inc(o_done, 1)

            def batch(b, last_batch):
                transpose_and_k(b, 0, 1, 0, 0)
                for c in range(CC):
                    mm(psG[:, c, :], zeros[:], esel[:, 0:4, :], start=True, stop=False)
                query(b, 0, 1, HEAD, 0)
                query(b, 0, 1, HEAD, 1)
                def step(t, par):
                    transpose_and_k(b, 2 * t - 1, par, 1, 0)
                    gram(b, 2 * t - 2, 0)
                    pe.wait_ge(xl_ready, PRIME + NHB * b + 2 * t + 1)
                    query(b, t, par, BLK, 0)
                    transpose_and_k(b, 2 * t, par, 0, HALF)
                    gram(b, 2 * t - 1, 1)
                    query(b, t, par, BLK, 1)
                with pe.Fori(0, 5) as i:
                    step(2 * i + 1, 0)
                    step(2 * i + 2, 1)
                step(NBLK - 2, 0)
                t = NBLK - 1
                transpose_and_k(b, 2 * t - 1, 1, 1, 0)
                gram(b, 2 * t - 2, 0)
                transpose_and_k(b, 2 * t, 1, 0, HALF)
                gram(b, 2 * t - 1, 1)
                query(b, t, 1, BLK, 0)
                query(b, t, 1, BLK, 1)
                pe.wait_ge(kacc_done, PRIME + NHB * (b + 1))
                for c in range(CC):
                    for i in range(TILES):
                        last = mm(psK[:, 0, c:c + 1], kacc[:, i, c * P:(c + 1) * P], ones[:],
                                  start=(i == 0), stop=(i == TILES - 1))
                last.then_inc(ksum_done, 1)
                gram(b, NHB - 1, 0, stop=True)
                pe.wait_ge(swin_ready, b + 1)
                pe.wait_ge(q_saved, CC * NBLK * (b + 1) - 2)
                denominators(0, 0, 2)
                pe.wait_ge(gt_ready, b + 1)
                for c in range(CC):
                    for i in range(CC):
                        last = mm(psK[:, 1, c * P:(c + 1) * P], wv[:, i, c * P:(c + 1) * P],
                                  posb[:, 0, i * C + c * P:i * C + (c + 1) * P], start=(i == 0), stop=(i == CC - 1))
                last.then_inc(kv_done, 1)
                denominators(0, 2, GRP0)
                pe.wait_ge(kvm_ready, b + 1)
                for c in range(CC):
                    last = mm(psQ[:, 0, c * C:(c + 1) * C], posb[:, 1, c * P:(c + 1) * P], pw[:, c, :],
                              start=True, stop=True)
                last.then_inc(m_done, 1)
                pe.wait_ge(q_saved, CC * NBLK * (b + 1))
                denominators(1, 0, 4)
                spread_z(b, 0)
                denominators(1, 4, 5)
                spread_z(b, 1)
                denominators(1, 5, NBLK - GRP0)
                pe.wait_ge(ml_ready, b + 1)
                for t in range(2, NBLK):
                    spread_z(b, t)
                    output(b, t - 2)
                    if not last_batch and t == 10:
                        gn_group_mean(b + 1)
                    if not last_batch and t == 11:
                        gn_group_var(b + 1)
                output(b, NBLK - 2)
                output(b, NBLK - 1)

            with pe.Fori(0, B - 1) as b:
                batch(b, False)
            batch(B - 1, True)

        @block.vector
        def _(dve):
            v = nc.vector

            def x_stats(b, t, n):
                for c in range(CC):
                    last = v.bn_stats(stats[:, c, t, :], ring[:, slot(b, t), c, 0:n])
                last.then_inc(stats_done, 1)

            def gn_channels(b):
                dve.wait_ge(stats_done, NBLK * (b + 1))
                v.tensor_copy(landing[:], stats[:, 0, 0, 0:2])
                for c in range(CC):
                    last = v.bn_aggr(mv[:, c, :], stats[:, c, :, :].rearrange("p t s -> p (t s)"))
                last.then_inc(gn_step, 1)

            def gn_offsets(b):
                dve.wait_ge(gn_mean, b + 1)
                dve.wait_ge(gn_step, 10 * b + 1)
                v.tensor_copy(gmean[:], psT[:, 0, 0:CC])
                v.tensor_tensor(gdev[:], mv[:, :, 0], psT[:, 0, 0:CC], ALU.subtract).then_inc(gn_step, 1)
                dve.wait_ge(gn_step, 10 * b + 2)
                v.tensor_tensor(gtmp[:], gdev[:], gdev[:], ALU.mult).then_inc(gn_step, 1)
                dve.wait_ge(gn_step, 10 * b + 3)
                v.tensor_tensor(gvar[:], gtmp[:], mv[:, :, 1], ALU.add).then_inc(gn_step, 1)

            def gn_rstd(b):
                dve.wait_ge(gn_var, b + 1)
                v.tensor_scalar(gvar[:], psT[:, 0, 0:CC], GN_EPS, None, ALU.add).then_inc(gn_step, 1)
                dve.wait_ge(gn_sqrt, b + 1)
                v.reciprocal(rstd[:], gtmp[:]).then_inc(gn_step, 1)
                dve.wait_ge(gn_step, 10 * b + 6)
                v.tensor_tensor(gdev[:], rstd[:], rstd[:], ALU.mult).then_inc(gn_step, 1)
                dve.wait_ge(gn_step, 10 * b + 7)
                v.tensor_tensor(gdev[:], gdev[:], gvar[:], ALU.mult).then_inc(gn_step, 1)
                dve.wait_ge(gn_step, 10 * b + 8)
                v.tensor_scalar(gdev[:], gdev[:], -0.5, 1.5, ALU.mult, ALU.add).then_inc(gn_step, 1)
                dve.wait_ge(gn_step, 10 * b + 9)
                v.tensor_tensor(rstd[:], rstd[:], gdev[:], ALU.mult).then_inc(gn_step, 1)
                dve.wait_ge(gn_step, 10 * b + 10)

            def normalise(b, t, h, hp, tok):
                n = NHB * b + h
                if isinstance(h, int) and h == 0:
                    if not (isinstance(b, int) and b == 0):
                        dve.wait_ge(t_done, PRIME + n)
                        dve.wait_ge(xh_ready, PRIME + n)
                        dve.wait_ge(xl_ready, PRIME + n)
                else:
                    dve.wait_ge(t_done, PRIME + n - 1)
                    dve.wait_ge(xh_ready, PRIME + n - 1)
                    dve.wait_ge(xl_ready, PRIME + n - 1)
                for c in range(CC):
                    last = v.tensor_scalar(xn[:, hp, c, :], ring[:, slot(b, t), c, tok:tok + HALF],
                                           gmean[:, c:c + 1], rstd[:, c:c + 1], ALU.subtract, ALU.mult)
                last.then_inc(xn_ready, 1)

            def key_rest(b, h, hp, between=lambda: None):
                n = NHB * b + h
                dve.wait_ge(k_done, n + 1)
                dve.wait_ge(pos_loaded, 16 * (n + 1))
                dve.wait_ge(kacc_done, PRIME + n)
                dve.wait_ge(kl_ready, PRIME + n)
                v.tensor_tensor(kt[:], psK[:, hp, :], posb[:, hp, :], ALU.add).then_inc(kt_ready, 1)
                dve.wait_ge(xth_ready, n + 1)
                v.tensor_tensor(xt[:, hp, 1, :, :].rearrange("p i n -> p (i n)"), psT[:, hp, :],
                                xt[:, hp, 0, :, :].rearrange("p i n -> p (i n)"), ALU.subtract).then_inc(xtl_ready, 1)
                between()
                dve.wait_ge(kh_ready, n + 1)
                v.tensor_tensor(kk[:, hp, :, 1, :], kt[:].rearrange("p (i n) -> p i n", i=TILES), kk[:, hp, :, 0, :],
                                ALU.subtract).then_inc(kl_ready, 1)

            def invert(b, g, lo, hi):
                step = lo // (BLK // 4) * 2 if g else 0
                if lo == 0:
                    dve.wait_ge(den_done, 2 * b + g + 1)
                v.tensor_scalar(kt[0:64, lo:hi], psT[0:64, g, lo:hi], Z_EPS, None, ALU.add).then_inc(zt_step, 1)
                dve.wait_ge(zt_step, 10 * b + 2 * g + step + 1)
                v.reciprocal(kt[0:64, lo:hi], kt[0:64, lo:hi]).then_inc(zt_step, 1)
                if hi == BLK:
                    dve.wait_ge(zh_ready, 2 * b + g + 1)
                    v.tensor_tensor(zhl[64:128, g, :], kt[0:64, :], zhl[0:64, g, :], ALU.subtract).then_inc(zl_ready, 1)

            def scale_q(b, t, n):
                dve.wait_ge(zb_done, NBLK * b + t + 1)
                v.tensor_tensor(q[:, :, cols(t, n)], q[:, :, cols(t, n)], psG[:, :, 0:n], ALU.mult).then_inc(u_ready, 1)

            def residual(b, t, n, psO):
                for m in range(CC):
                    dve.wait_ge(o_done, PRIME + CC * (NBLK * b + t) + m + 1)
                    xs = ring[:, slot(b, t), m, 0:n]
                    v.scalar_tensor_tensor(out=xs, in0=psO[:, m, 0:n], scalar=pb[:, m:m + 1], in1=xs,
                                           op0=ALU.add, op1=ALU.add).then_inc(out_ready, 1)

            v.memset(ones[:], 1.0)
            v.memset(kacc[:], 0.0).then_inc(kacc_zero, 1)
            v.memset(swin[:], 0.0)
            v.memset(zeros[:].bitcast(F32), 0.0)
            dve.wait_ge(w_loaded, 16 * 13)
            for c in range(CC):
                last = v.tensor_scalar(bvm[:, c, :], bmask[:], bv[:, c:c + 1], None, ALU.mult)
            last.then_inc(bvm_ready, 1)
            v.tensor_copy(esel[:], esel_raw)
            v.tensor_copy(wqk[:, 0, :, :], wqk_raw).then_inc(w_high, 1)
            dve.wait_ge(w_high, 1)
            v.tensor_tensor(wqk[:, 1, :, :], wqk_raw, wqk[:, 0, :, :], ALU.subtract)
            dve.wait_ge(bpb_done, 1)
            v.tensor_copy(bpb[:].rearrange("p c n -> p (c n)"), psK[:, 0, :]).then_inc(setup_done, 1)
            for k in range(PIECES):
                dve.wait_ge(pos_raw[k % 2], 16 * (k // 2 + 1))
                for h in range(PH):
                    seg = piece[k % 2][:, h * TILES * C:(h + 1) * TILES * C]
                    last = v.tensor_tensor(seg, seg, bk_b, ALU.add)
                last.then_inc(pos_added, 1)
            for t in range(NBLK):
                dve.wait_ge(x_first[t % 4], 16 * (t // 4 + 1))
                x_stats(0, t, BLK if t else HEAD)
            gn_channels(0)
            gn_offsets(0)
            gn_rstd(0)
            normalise(0, 0, 0, 0, 0)

            def batch(b, last_batch):
                def pair(t, with_stats):
                    key_rest(b, 2 * t - 2, 0, lambda: normalise(b, t, 2 * t, 0, HALF))
                    if isinstance(t, int) and t == NBLK - 1:
                        key_rest(b, 2 * t - 1, 1)
                    else:
                        key_rest(b, 2 * t - 1, 1, lambda: normalise(b, t + 1, 2 * t + 1, 1, 0))
                    if with_stats:
                        dve.wait_ge(x_loaded, PRIME_DMA + 16 * (NBLK * b + t - NBLK + EARLY + 1))
                        x_stats(b + 1, t - NBLK + EARLY, BLK)
                normalise(b, 1, 1, 1, 0)
                with dve.Fori(0, 2) as i:
                    pair(2 * i + 1, False)
                    pair(2 * i + 2, False)
                if not last_batch:
                    dve.wait_ge(x_loaded, PRIME_DMA + 16 * (NBLK * b + 1))
                    x_stats(b + 1, 0, HEAD)
                with dve.Fori(2, 5) as i:
                    pair(2 * i + 1, not last_batch)
                    pair(2 * i + 2, not last_batch)
                pair(NBLK - 2, not last_batch)
                pair(NBLK - 1, not last_batch)
                key_rest(b, NHB - 1, 0)
                dve.wait_ge(ksum_done, b + 1)
                v.tensor_copy(ksc[:], psK[:, 0, 0:CC]).then_inc(ksc_ready, 1)
                dve.wait_ge(ksc_ready, b + 1)
                for c in range(CC):
                    s = WIN + 32 * c
                    last = v.tensor_scalar(swin[:, c, s:s + HPC], hmask[:], ksc[:, c:c + 1], None, ALU.mult)
                last.then_inc(swin_ready, 1)
                v.memset(kacc[:], 0.0).then_inc(kacc_zero, 1)
                gt = posb[:, 0, :].rearrange("p (c n) -> p c n", c=CC)
                dve.wait_ge(gl_copied, b + 1)
                v.tensor_tensor(gt, psG[:, :, 0:C], gt, ALU.add).then_inc(gt_ready, 1)
                dve.wait_ge(kv_done, b + 1)
                for c in range(CC):
                    last = v.tensor_tensor(posb[:, 1, c * P:(c + 1) * P], psK[:, 1, c * P:(c + 1) * P], bmask[:], ALU.mult)
                last.then_inc(kvm_ready, 1)
                dve.wait_ge(m_done, b + 1)
                for c in range(CC):
                    last = v.scalar_tensor_tensor(out=posb[:, 0, c * C:(c + 1) * C], in0=bpb[:, c, :], scalar=ksc[:, c:c + 1],
                                                  in1=psQ[:, 0, c * C:(c + 1) * C], op0=ALU.mult, op1=ALU.add)
                last.then_inc(m_sum, 1)
                dve.wait_ge(mh_ready, b + 1)
                v.tensor_tensor(mhl[:, 1, :, :].rearrange("p c n -> p (c n)"), posb[:, 0, :],
                                mhl[:, 0, :, :].rearrange("p c n -> p (c n)"), ALU.subtract).then_inc(ml_ready, 1)
                invert(b, 0, 0, BLK)
                scale_q(b, 0, HEAD)
                scale_q(b, 1, BLK)
                for t in range(2, NBLK):
                    scale_q(b, t, BLK)
                    residual(b, t - 2, BLK if t > 2 else HEAD, psK if t % 2 else psQ)
                    if 2 <= t <= 5:
                        invert(b, 1, (t - 2) * BLK // 4, (t - 1) * BLK // 4)
                    if not last_batch:
                        if t in STATS_AT:
                            k = EARLY + STATS_AT.index(t)
                            dve.wait_ge(x_loaded, PRIME_DMA + 16 * (NBLK * b + k + 1))
                            x_stats(b + 1, k, BLK)
                        if t == 9:
                            gn_channels(b + 1)
                        if t == 10:
                            gn_offsets(b + 1)
                        if t == 11:
                            gn_rstd(b + 1)
                        if t == 12:
                            normalise(b + 1, 0, 0, 0, 0)
                residual(b, NBLK - 2, BLK, psK)
                residual(b, NBLK - 1, BLK, psQ)

            with dve.Fori(0, B - 1) as b:
                batch(b, False)
            batch(B - 1, True)

        @block.scalar
        def _(act):
            a = nc.scalar.activation

            def gn_root(b):
                act.wait_ge(gn_step, 10 * b + 5)
                a(gtmp[:], gvar[:], ACT.Sqrt).then_inc(gn_sqrt, 1)

            def xn_high(b, h, par, hp, tok, free):
                act.wait_ge(xn_ready, NHB * b + h + 1)
                free(act)
                a(hl[:, par, 0, :, tok:tok + HALF], xn[:, hp, :, :], ACT.Copy).then_inc(xh_ready, 1)

            def rest(b, h, hp):
                n = NHB * b + h
                act.wait_ge(t_done, PRIME + n + 1)
                if isinstance(h, int) and h == 0:
                    act.wait_ge(g_done, PRIME + n)
                else:
                    act.wait_ge(g_done, PRIME + n - 1)
                a(xt[:, hp, 0, :, :].rearrange("p i n -> p (i n)"), psT[:, hp, :], ACT.Copy).then_inc(xth_ready, 1)
                act.wait_ge(kt_ready, PRIME + n + 1)
                a(kt[:], kt[:], ACT.Relu).then_inc(kr_ready, 1)
                act.wait_ge(kr_ready, n + 1)
                a(kk[:, hp, :, 0, :], kt[:].rearrange("p (i n) -> p i n", i=TILES), ACT.Copy).then_inc(kh_ready, 1)

            def save_q(b, t, n, m):
                act.wait_ge(q_done, CC * (NBLK * b + t) + m + 1)
                a(q[:, m, cols(t, n)], psQ[:, m, 0:n], ACT.Relu, bias=bq[:, m:m + 1]).then_inc(q_saved, 1)

            def block_free(b, t):
                return lambda eng: eng.wait_ge(q_done, CC * (NBLK * b + t - 1))

            def phase_free(b, k):
                return lambda eng: eng.wait_ge(o_done, PRIME + CC * (NBLK * b + k))

            def z_high(b, g):
                act.wait_ge(zt_step, 10 * b + 8 * g + 2)
                a(zhl[0:64, g, :], kt[0:64, :], ACT.Copy).then_inc(zh_ready, 1)

            def u_high(b, t, n, buf):
                act.wait_ge(u_ready, NBLK * b + t + 1)
                if not (isinstance(t, int) and t < 3):
                    act.wait_ge(o_done, PRIME + CC * (NBLK * b + t - 2))
                a(ubuf[buf][:, 0, :, 0:n], q[:, :, cols(t, n)], ACT.Copy).then_inc(uh_ready, 1)

            gn_root(0)
            xn_high(0, 0, 1, 0, 0, lambda eng: None)

            def batch(b, last_batch):
                xn_high(b, 1, 0, 1, 0, phase_free(b, 0))
                rest(b, 0, 0)
                save_q(b, 0, HEAD, 0)
                save_q(b, 0, HEAD, 1)

                def step(t, par):
                    xn_high(b, 2 * t, par, 0, HALF, lambda eng: None)
                    rest(b, 2 * t - 1, 1)
                    save_q(b, t, BLK, 0)
                    if not (isinstance(t, int) and t == NBLK - 1):
                        xn_high(b, 2 * t + 1, 1 - par, 1, 0, block_free(b, t + 1))
                    rest(b, 2 * t, 0)
                    save_q(b, t, BLK, 1)
                with act.Fori(0, 5) as i:
                    step(2 * i + 1, 0)
                    step(2 * i + 2, 1)
                step(NBLK - 2, 0)
                step(NBLK - 1, 1)
                act.wait_ge(g_done, PRIME + NHB * (b + 1))
                act.wait_ge(kt_ready, PRIME + NHB * (b + 1))
                a(posb[:, 0, :].rearrange("p (c n) -> p c n", c=CC), psG[:, :, C:2 * C], ACT.Copy).then_inc(gl_copied, 1)
                act.wait_ge(m_sum, b + 1)
                a(mhl[:, 0, :, :].rearrange("p c n -> p (c n)"), posb[:, 0, :], ACT.Copy).then_inc(mh_ready, 1)
                z_high(b, 0)
                u_high(b, 0, HEAD, 0)
                for t in (1, 2, 3, 4, 5):
                    u_high(b, t, BLK, t % 3)
                z_high(b, 1)
                u_high(b, 6, BLK, 0)
                with act.Fori(2, 3) as i:
                    for s in (1, 2, 3):
                        u_high(b, 3 * i + s, BLK, s % 3)
                u_high(b, 10, BLK, 1)
                if not last_batch:
                    gn_root(b + 1)
                u_high(b, 11, BLK, 2)
                u_high(b, 12, BLK, 0)
                if not last_batch:
                    xn_high(b + 1, 0, 1, 0, 0, phase_free(b, NBLK - 2))

            with act.Fori(0, B - 1) as b:
                batch(b, False)
            batch(B - 1, True)

        @block.gpsimd
        def _(pool):
            g = nc.gpsimd

            def xn_low(b, h, par, hp, tok):
                pool.wait_ge(xh_ready, PRIME + NHB * b + h + 1)
                g.tensor_tensor(hl[:, par, 1, :, tok:tok + HALF], xn[:, hp, :, :], hl[:, par, 0, :, tok:tok + HALF],
                                ALU.subtract).then_inc(xl_ready, 1)

            def key_sum(b, h):
                n = NHB * b + h
                pool.wait_ge(kr_ready, n + 1)
                pool.wait_ge(kacc_zero, b + 1)
                pool.wait_ge(kacc_done, PRIME + n)
                g.tensor_tensor(kacc[:].rearrange("p i n -> p (i n)"), kacc[:].rearrange("p i n -> p (i n)"), kt[:],
                                ALU.add).then_inc(kacc_done, 1)

            def u_low(b, t, n, buf):
                pool.wait_ge(uh_ready, NBLK * b + t + 1)
                g.tensor_tensor(ubuf[buf][:, 1, :, 0:n], q[:, :, cols(t, n)], ubuf[buf][:, 0, :, 0:n],
                                ALU.subtract).then_inc(ul_ready, 1)

            for s in primed:
                pool.sem_inc(s, PRIME)
            for s in primed_dma:
                pool.sem_inc(s, PRIME_DMA)
            xn_low(0, 0, 1, 0, 0)

            def batch(b, last_batch):
                with pool.Fori(0, 6) as i:
                    for s in (1, 2):
                        t = 2 * i + s
                        par = (s + 1) % 2
                        xn_low(b, 2 * t - 1, par, 1, 0)
                        key_sum(b, 2 * t - 2)
                        xn_low(b, 2 * t, par, 0, HALF)
                        key_sum(b, 2 * t - 1)
                key_sum(b, NHB - 1)
                u_low(b, 0, HEAD, 0)
                with pool.Fori(0, 4) as i:
                    for s in (1, 2, 3):
                        u_low(b, 3 * i + s, BLK, s % 3)
                if not last_batch:
                    xn_low(b + 1, 0, 1, 0, 0)

            with pool.Fori(0, B - 1) as b:
                batch(b, False)
            batch(B - 1, True)


def kernel(**inputs):
    import concourse.bacc as bacc
    from concourse.bass_utils import run_bass_kernel_spmd

    x = np.ascontiguousarray(inputs["x"])
    qkv_w = np.asarray(inputs["L0_conv_qkv_w"])
    qkv_b = np.asarray(inputs["L0_conv_qkv_b"])
    proj_w = np.asarray(inputs["L0_conv_proj_w"])
    proj_b = np.asarray(inputs["L0_conv_proj_b"])
    chan = np.arange(P)
    same_head = (chan[:, None] // HD == chan[None, :] // HD)
    row = 32 * np.arange(CC)[None, :, None] + 4 * np.arange(GRP0)[:, None, None] + (chan // HD)[None, None, :]
    esel = (np.arange(P)[:, None, None, None] % 64 == row[None]).reshape(P, GRP0 * CC, P)
    arrays = {
        "x": x.reshape(B, CC, P, N),
        "wqk": np.ascontiguousarray(qkv_w[:2 * C].T).reshape(CC, P, 2 * C),
        "wv": np.ascontiguousarray(qkv_w[2 * C:].T).reshape(CC, P, C),
        "pw": np.ascontiguousarray(proj_w.T).reshape(CC, P, C),
        "bq": np.ascontiguousarray(qkv_b[:C].reshape(CC, P).T),
        "bk": np.ascontiguousarray(qkv_b[C:2 * C].reshape(1, C)),
        "bv": np.ascontiguousarray(qkv_b[2 * C:].reshape(CC, P).T),
        "pb": np.ascontiguousarray(proj_b.reshape(CC, P).T),
        "pos": np.ascontiguousarray(np.asarray(inputs["L0_conv_pos_enc"]).reshape(N, C)),
        "ident": np.eye(P, dtype=np.float32),
        "gavg": (chan[:, None] // GROUP == chan[None, :] // GROUP).astype(np.float32) / GROUP,
        "hmask": (chan[:, None] // HD == np.arange(HPC)[None, :]).astype(np.float32),
        "bmask": same_head.astype(np.float32),
        "esel": esel.astype(np.float32),
    }
    arrays = {f"in_{name}": a for name, a in arrays.items()}
    nc = bacc.Bacc("TRN2", target_bir_lowering=False, num_devices=1)
    f32 = mybir.dt.float32
    args = [nc.dram_tensor(name, a.shape, f32, kind="ExternalInput").ap() for name, a in arrays.items()]
    posb = nc.dram_tensor("pos_plus_bk", (NHB, P, TILES * C), f32, kind="Internal").ap()
    y = nc.dram_tensor("y", (B, CC, P, N), f32, kind="ExternalOutput").ap()
    build(nc, *args, posb, y)
    r = run_bass_kernel_spmd(nc, [arrays], core_ids=[0])
    return r.results[0]["y"].reshape(B, C, H, W)
```

```python
from contextlib import ExitStack

import numpy as np

import concourse.bass as bass
from concourse import mybir

B, C, H, W = 16, 256, 80, 80
N = H * W
HEADS = 8
HD = C // HEADS
P = 128
CC = C // P
GROUP = C // 32
BLK = 512
HALF = BLK // 2
TILES = HALF // P
HEAD = N % BLK
NBLK = 1 + N // BLK
NHB = N // HALF
HPC = P // HD
SLOTS = 22
EARLY = SLOTS - NBLK
GRP0 = 5
GRP1 = NBLK - GRP0
WIN0, WIN1 = 4 * (GRP0 - 1), 4 * (GRP1 - 1)
LOW_BY_DVE = 3
LAG = 2
STATS_AT = (6, 7, 7, 8, 9, 9, 10, 11)
PRIME, PRIME_DMA = 5, 16
GN_EPS = 1e-5
Z_EPS = 1e-6


def build(nc, x, wqk_d, wv_d, pw_d, bq_d, bk_d, bv_d, pb_d, pos, ident_d, gavg_d, hmask_d, bmask_d, esel_d, posb_d, y):
    F32 = mybir.dt.float32
    F32R = mybir.dt.float32r
    ALU = mybir.AluOpType
    ACT = mybir.ActivationFunctionType
    ctx = ExitStack()
    with ctx:
        def sb(name, shape, dt=F32):
            return ctx.enter_context(nc.sbuf_tensor(name, shape, dt))

        def ps(name, shape):
            return ctx.enter_context(nc.psum_tensor(name, shape, F32))

        def sem(name):
            return ctx.enter_context(nc.semaphore(name))

        ring = sb("ring", [P, SLOTS, CC, BLK])
        q = sb("q", [P, CC, N])
        hl = sb("hl", [P, 2, 2, CC, BLK], F32R)
        xn = sb("xn", [P, 2, CC, HALF])
        xt = sb("xt", [P, 2, 2, TILES, C], F32R)
        kk = sb("kk", [P, 2, TILES, 2, C], F32R)
        kt = sb("kt", [P, TILES * C])
        posb = sb("posb", [P, 2, TILES * C])
        kacc = sb("kacc", [P, TILES, C])
        wqk = sb("wqk", [P, 2, CC, 2 * C], F32R)
        wv = sb("wv", [P, CC, C])
        pw = sb("pw", [P, CC, C])
        bpb = sb("bpb", [P, CC, C])
        esel = sb("esel", [P, GRP1 * CC, P], F32R)
        xtu = xt[:].rearrange("p a l i n -> p (a l) (i n)").rearrange("p (l c) n -> p l c n", l=2)
        ubuf = [hl[:, 0], hl[:, 1], xtu]
        mhl = kk[:, 0, :, :, :]
        zhl = kk[:, 1, :, :, :].rearrange("p i a n -> p i (a n)")
        swin = sb("swin", [P, CC, WIN0 + 64])
        swr = sb("swr", [P, CC, WIN1 + P], F32R)
        ident = sb("ident", [P, P])
        gavg = sb("gavg", [P, P])
        hmask = sb("hmask", [P, HPC])
        consts = sb("consts", [P, 2])
        ones, zeps = consts[:, 0:1], consts[:, 1:2]
        biases = sb("biases", [P, 3, CC])
        bq, bv, pb = (biases[:, i, :] for i in range(3))
        ksc = sb("ksc", [P, CC])
        stats = sb("stats", [P, CC, NBLK, 6])
        mv = sb("mv", [P, CC, 2])
        landing = sb("landing", [P, 2])
        gmean = sb("gmean", [P, CC])
        gdev = sb("gdev", [P, CC])
        gvar = sb("gvar", [P, CC])
        gtmp = sb("gtmp", [P, CC])
        rstd = sb("rstd", [P, CC])

        psG = ps("psG", [P, CC, BLK])
        psT = ps("psT", [P, 2, BLK])
        psK = ps("psK", [P, 2, BLK])
        psQ = ps("psQ", [P, 2, BLK])

        out_banks = [psQ, psT, psK]

        w_loaded = sem("w_loaded")
        x_first = [sem(f"x_first{i}") for i in range(4)]
        pos_added = sem("pos_added")
        pos_stored = sem("pos_stored")
        x_loaded = sem("x_loaded")
        pos_loaded = sem("pos_loaded")
        stored = [sem("stored_even"), sem("stored_odd")]
        w_high = sem("w_high")
        bvm_ready = sem("bvm_ready")
        bpb_done = sem("bpb_done")
        setup_done = sem("setup_done")
        stats_done = sem("stats_done")
        gn_step = sem("gn_step")
        gn_mean = sem("gn_mean")
        gn_var = sem("gn_var")
        gn_sqrt = sem("gn_sqrt")
        xn_ready = sem("xn_ready")
        xh_ready = sem("xh_ready")
        xl_ready = sem("xl_ready")
        t_done = sem("t_done")
        k_done = sem("k_done")
        g_done = sem("g_done")
        q_done = sem("q_done")
        xth_ready = sem("xth_ready")
        xtl_ready = sem("xtl_ready")
        kt_ready = sem("kt_ready")
        kr_ready = sem("kr_ready")
        kh_ready = sem("kh_ready")
        kl_ready = sem("kl_ready")
        kacc_zero = sem("kacc_zero")
        kacc_done = sem("kacc_done")
        q_saved = sem("q_saved")
        ksum_done = sem("ksum_done")
        ksc_ready = sem("ksc_ready")
        swin_ready = sem("swin_ready")
        swr_step = sem("swr_step")
        qh_ready = sem("qh_ready")
        ql_ready = sem("ql_ready")
        ql_dve = sem("ql_dve")
        qs_used = sem("qs_used")
        gl_copied = sem("gl_copied")
        gt_ready = sem("gt_ready")
        kv_done = sem("kv_done")
        kvm_zero = sem("kvm_zero")
        kvm_ready = sem("kvm_ready")
        m_done = sem("m_done")
        m_sum = sem("m_sum")
        mh_ready = sem("mh_ready")
        ml_ready = sem("ml_ready")
        den_done = sem("den_done")
        zt_step = sem("zt_step")
        zh_ready = sem("zh_ready")
        zl_ready = sem("zl_ready")
        zb_done = sem("zb_done")
        u_ready = sem("u_ready")
        uh_ready = sem("uh_ready")
        ul_ready = sem("ul_ready")
        o_done = sem("o_done")
        out_ready = sem("out_ready")

        wqk_raw = q[:, 0, 0:CC * 2 * C].rearrange("p (c n) -> p c n", c=CC)
        esel_raw = q[:, 0, 2048:2048 + GRP1 * CC * P].rearrange("p (j n) -> p j n", n=P)
        bmask = q[:, 1, CC * P:(CC + 1) * P]
        bvm = q[:, 1, 0:CC * P].rearrange("p (c n) -> p c n", c=CC)
        bk_b = ring[:, 0, :, HEAD:BLK]

        def start(t):
            return HEAD + (t - 1) * BLK

        def slot(b, t):
            return (NBLK * b + t) % SLOTS

        def cols(t, n):
            return bass.ds(0 if n == HEAD else start(t), n)

        def z_bank(t):
            return psK if t in (1, 3) else psG

        def stored_before(b, t, par):
            return PRIME_DMA + (16 * (NBLK // 2 + 1 - par)) * b + 8 * (t - par)

        block = ctx.enter_context(nc.Block())

        primed = [xtl_ready, kt_ready, out_ready, t_done, xh_ready, xl_ready, kacc_done, kl_ready, g_done, o_done]
        primed_dma = [x_loaded] + stored

        @block.sync
        def _(sp):
            smalls = [(wqk_raw, wqk_d.rearrange("c p n -> p c n")), (esel_raw, esel_d), (wv[:], wv_d.rearrange("c p n -> p c n")),
                      (pw[:], pw_d.rearrange("c p n -> p c n")), (ident[:], ident_d), (gavg[:], gavg_d),
                      (bmask, bmask_d), (hmask[:], hmask_d), (bq[:], bq_d), (bv[:], bv_d), (pb[:], pb_d)]

            def load_x(b, t, n):
                return sp.dma_start(ring[:, slot(b, t), :, 0:n],
                                    x[b, :, :, cols(t, n)].rearrange("c p n -> p c n"))

            for t in range(NBLK):
                if t >= 4:
                    sp.wait_ge(x_first[t % 4], 16 * (t // 4))
                load_x(0, t, HEAD if t == 0 else BLK).then_inc(x_first[t % 4], 16)
                if t == 3:
                    for dst, src in smalls:
                        sp.dma_start(dst, src).then_inc(w_loaded, 16)
                    for i in range(TILES):
                        sp.dma_start(bk_b[:, i, :], bk_d.partition_broadcast(P)).then_inc(w_loaded, 16)

            def load_raw_pos(h):
                if h >= 2:
                    sp.wait_ge(kt_ready, PRIME + h - 1)
                    sp.wait_ge(pos_stored, 16 * (h - 1))
                if h:
                    sp.wait_ge(pos_loaded, 16 * h)
                sp.dma_start(posb[:, h % 2, :], pos[h, :, :]).then_inc(pos_loaded, 16)

            def store_pos(h):
                sp.wait_ge(pos_added, h + 1)
                if h:
                    sp.wait_ge(pos_stored, 16 * h)
                sp.dma_start(posb_d[h, :, :], posb[:, h % 2, :]).then_inc(pos_stored, 16)

            def load_pos_at(b, h, parity):
                sp.wait_ge(kt_ready, PRIME + NHB * b + h - 1)
                sp.wait_ge(pos_loaded, (16 * NHB) * b + 16 * h)
                sp.dma_start(posb[:, parity, :], posb_d[h, :, :]).then_inc(pos_loaded, 16)

            def load_next_x(b, t, n):
                sp.wait_ge(x_loaded, PRIME_DMA + 16 * (NBLK * b + t))
                load_x(b + 1, t, n).then_inc(x_loaded, 16)

            def store_y(b, t, n, par):
                sp.wait_ge(out_ready, PRIME + CC * (NBLK * b + t + 1))
                sp.wait_ge(stored[par], stored_before(b, t, par))
                sp.dma_start(y[b, :, :, cols(t, n)].rearrange("c p n -> p c n"),
                             ring[:, slot(b, t), :, 0:n]).then_inc(stored[par], 16)

            def first_phase_a():
                for h in range(NHB):
                    store_pos(h)
                    if h + 2 < NHB:
                        load_raw_pos(h + 2)
                    early = h - (NHB - 2 * EARLY - 2)
                    if early in range(0, 2 * EARLY, 2):
                        load_next_x(0, early // 2, BLK if early else HEAD)

            def phase_a(b, last):
                with sp.Fori(0, NBLK - 1 - EARLY) as i:
                    load_pos_at(b, 2 * i + 2, 0)
                    load_pos_at(b, 2 * i + 3, 1)
                if not last:
                    for par in range(2):
                        sp.wait_ge(stored[par], stored_before(b, par, par))
                    load_next_x(b, 0, HEAD)
                with sp.Fori(0, EARLY - 1) as i:
                    load_pos_at(b, 2 * i + NHB - 1 - 2 * (EARLY - 1), 0)
                    load_pos_at(b, 2 * i + NHB - 2 * (EARLY - 1), 1)
                    if not last:
                        load_next_x(b, i + 1, BLK)
                load_pos_at(b, NHB - 1, 0)

            def phase_b(b, last):
                store_y(b, 0, HEAD, 0)
                with sp.Fori(0, (NBLK - EARLY) // 2) as i:
                    for s in (1, 2):
                        store_y(b, 2 * i + s, BLK, s % 2)
                        if not last:
                            sp.wait_ge(stored[1 - s % 2], stored_before(b, 2 * i + s + 1, 1 - s % 2))
                            load_next_x(b, 2 * i + s + EARLY - 1, BLK)
                if not last:
                    sp.wait_ge(ml_ready, b + 1)
                    for h in range(2):
                        sp.wait_ge(pos_loaded, 16 * (NHB * (b + 1) + h))
                        sp.dma_start(posb[:, h, :], posb_d[h, :, :]).then_inc(pos_loaded, 16)
                with sp.Fori((NBLK - EARLY) // 2, 6) as i:
                    for s in (1, 2):
                        store_y(b, 2 * i + s, BLK, s % 2)

            load_raw_pos(0)
            load_raw_pos(1)
            first_phase_a()
            sp.wait_ge(pos_stored, 16 * NHB)
            phase_b(0, False)
            with sp.Fori(1, B - 1) as b:
                phase_a(b, False)
                phase_b(b, False)
            phase_a(B - 1, True)
            phase_b(B - 1, True)
            for par in range(2):
                sp.wait_ge(stored[par], stored_before(B, par, par))

        @block.tensor
        def _(pe):
            mm = nc.tensor.matmul

            def gn_group_mean(b):
                pe.wait_ge(gn_step, 10 * b + 1)
                mm(psG[:, 0, 0:CC], gavg[:], mv[:, :, 0], start=True, stop=True).then_inc(gn_mean, 1)

            def gn_group_var(b):
                pe.wait_ge(gn_step, 10 * b + 4)
                mm(psG[:, 0, 0:CC], gavg[:], gvar[:], start=True, stop=True).then_inc(gn_var, 1)

            pe.wait_ge(bvm_ready, 1)
            for c in range(CC):
                last = mm(psK[:, 0, c * C:(c + 1) * C], bvm[:, c, :], pw[:, c, :], start=True, stop=True)
            last.then_inc(bpb_done, 1)
            gn_group_mean(0)
            gn_group_var(0)
            pe.wait_ge(setup_done, 1)

            def transpose_and_k(b, h, par, hp, tok):
                n = NHB * b + h
                pe.wait_ge(xh_ready, PRIME + n + 1)
                pe.wait_ge(xl_ready, PRIME + n + 1)
                if isinstance(h, int) and h == 0:
                    pe.wait_ge(out_ready, PRIME + CC * (NBLK * b - 2))
                else:
                    pe.wait_ge(xtl_ready, PRIME + n - 1)
                for i in range(TILES):
                    for c in range(CC):
                        last = nc.tensor.transpose(psT[:, hp, i * C + c * P:i * C + (c + 1) * P],
                                                   xn[:, hp, c, i * P:(i + 1) * P], ident[:])
                last.then_inc(t_done, 1)
                if isinstance(h, int) and h == 0:
                    pe.wait_ge(out_ready, PRIME + CC * (NBLK * b - 1))
                else:
                    pe.wait_ge(kt_ready, PRIME + n - 1)
                for i in range(TILES):
                    s = tok + i * P
                    terms = [(c, a, w) for c in range(CC) for a, w in ((0, 0), (0, 1), (1, 0))]
                    for j, (c, a, w) in enumerate(terms):
                        last = mm(psK[:, hp, i * C:(i + 1) * C], hl[:, par, a, c, s:s + P], wqk[:, w, c, C:2 * C],
                                  start=(j == 0), stop=(j == len(terms) - 1))
                last.then_inc(k_done, 1)

            def gram(b, h, hp, start=False, stop=False):
                n = NHB * b + h
                pe.wait_ge(xtl_ready, PRIME + n + 1)
                pe.wait_ge(kl_ready, PRIME + n + 1)
                for i in range(TILES):
                    for c in range(CC):
                        mm(psG[:, c, :], xt[:, hp, 0, i, c * P:(c + 1) * P], kk[:, hp, i, :, :],
                           start=start and i == 0, stop=False)
                        last = mm(psG[:, c, C:2 * C], xt[:, hp, 1, i, c * P:(c + 1) * P], kk[:, hp, i, 0, :],
                                  start=False, stop=stop and i == TILES - 1)
                last.then_inc(g_done, 1)

            def query(b, t, par, n, m):
                if n == HEAD:
                    pe.wait_ge(out_ready, PRIME + CC * NBLK * b - 1 + m)
                else:
                    pe.wait_ge(q_saved, CC * (NBLK * b + t) + m - 1)
                terms = [(c, a, w) for c in range(CC) for w, a in ((0, 0), (0, 1), (1, 0))]
                for j, (c, a, w) in enumerate(terms):
                    last = mm(psQ[:, m, 0:n], wqk[:, w, c, m * P:(m + 1) * P], hl[:, par, a, c, 0:n],
                              start=(j == 0), stop=(j == len(terms) - 1))
                last.then_inc(q_done, 1)

            def denominators_float(lo, hi):
                order = list(range(1, GRP0)) + [0]
                for t in order[lo:hi]:
                    n = BLK if t else HEAD
                    s = start(t) if t else 0
                    w = WIN0 - 4 * t
                    for c in range(CC):
                        last = mm(psT[0:64, 0, 0:n], swin[:, c, w:w + 64], q[:, c, s:s + n],
                                  start=(t == 1 and c == 0), stop=(t == 0 and c == CC - 1))
                if hi == GRP0:
                    last.then_inc(den_done, 1)

            def denominators_split(b, j):
                if j == LOW_BY_DVE:
                    pe.wait_ge(ql_dve, b + 1)
                else:
                    pe.wait_ge(ql_ready, (GRP1 - 1) * b + j + 1 - (j > LOW_BY_DVE))
                w = WIN1 - 4 * j
                final = j == GRP1 - 1
                for part in (1, 0) if final else (0, 1):
                    rows = 64 if part else P
                    for c in range(CC):
                        last = mm(psT[0:rows, 1, :], swr[:, c, w:w + rows], ubuf[j % 3][:, part, c, :],
                                  start=(j == 0 and part == 0 and c == 0), stop=(final and part == 0 and c == CC - 1))
                last.then_inc(qs_used, 1)

            def spread_z(b, t):
                n = BLK if t else HEAD
                g = 0 if t < GRP0 else 1
                if t in (0, GRP0):
                    pe.wait_ge(zl_ready, 2 * b + g + 1)
                if t >= 2:
                    pe.wait_ge(u_ready, NBLK * b + (t if t >= GRP0 else t - 1))
                for c in range(CC):
                    last = mm(z_bank(t)[:, c, 0:n], esel[:, (t - g * GRP0) * CC + c, :], zhl[:, g, 0:n],
                              start=True, stop=True)
                last.then_inc(zb_done, 1)

            def output(b, t, between=lambda: None):
                n = BLK if t else HEAD
                psO = out_banks[t % 3]
                pe.wait_ge(uh_ready, NBLK * b + t + 1)
                if t >= 3:
                    pe.wait_ge(out_ready, PRIME + CC * (NBLK * b + t - 2))
                for m in range(CC):
                    for j, (c, w) in enumerate([(c, w) for c in range(CC) for w in range(2)]):
                        mm(psO[:, m, 0:n], mhl[:, w, c, m * P:(m + 1) * P], ubuf[t % 3][:, 0, c, 0:n],
                           start=(j == 0), stop=False)
                    if m == 0:
                        between()
                pe.wait_ge(ul_ready, NBLK * b + t + 1)
                for m in range(CC):
                    for c in range(CC):
                        last = mm(psO[:, m, 0:n], mhl[:, 0, c, m * P:(m + 1) * P], ubuf[t % 3][:, 1, c, 0:n],
                                  start=False, stop=(c == CC - 1))
                    last.then_inc(o_done, 1)

            def batch(b, last_batch):
                transpose_and_k(b, 0, 1, 0, 0)
                query(b, 0, 1, HEAD, 0)
                query(b, 0, 1, HEAD, 1)
                def step(t, par):
                    transpose_and_k(b, 2 * t - 1, par, 1, 0)
                    gram(b, 2 * t - 2, 0, start=isinstance(t, int) and t == 1)
                    pe.wait_ge(xl_ready, PRIME + NHB * b + 2 * t + 1)
                    query(b, t, par, BLK, 0)
                    transpose_and_k(b, 2 * t, par, 0, HALF)
                    gram(b, 2 * t - 1, 1)
                    query(b, t, par, BLK, 1)
                step(1, 0)
                with pe.Fori(0, 5) as i:
                    step(2 * i + 2, 1)
                    step(2 * i + 3, 0)
                t = NBLK - 1
                transpose_and_k(b, 2 * t - 1, 1, 1, 0)
                gram(b, 2 * t - 2, 0)
                transpose_and_k(b, 2 * t, 1, 0, HALF)
                gram(b, 2 * t - 1, 1)
                query(b, t, 1, BLK, 0)
                query(b, t, 1, BLK, 1)
                pe.wait_ge(kacc_done, PRIME + NHB * (b + 1))
                for c in range(CC):
                    for i in range(TILES):
                        last = mm(psK[:, 0, c:c + 1], kacc[:, i, c * P:(c + 1) * P], ones[:],
                                  start=(i == 0), stop=(i == TILES - 1))
                last.then_inc(ksum_done, 1)
                gram(b, NHB - 1, 0, stop=True)
                pe.wait_ge(swin_ready, b + 1)
                pe.wait_ge(q_saved, CC * NBLK * (b + 1) - 2)
                pe.wait_ge(swr_step, 2 * b + 2)
                denominators_split(b, 0)
                denominators_float(0, 1)
                denominators_split(b, 1)
                denominators_float(1, 2)
                pe.wait_ge(gt_ready, b + 1)
                for c in range(CC):
                    for i in range(CC):
                        last = mm(psK[:, 1, c * P:(c + 1) * P], wv[:, i, c * P:(c + 1) * P],
                                  posb[:, 0, i * C + c * P:i * C + (c + 1) * P], start=(i == 0), stop=(i == CC - 1))
                last.then_inc(kv_done, 1)
                denominators_split(b, 2)
                denominators_split(b, 3)
                denominators_float(2, GRP0)
                pe.wait_ge(kvm_ready, b + 1)
                for c in range(CC):
                    last = mm(psQ[:, 0, c * C:(c + 1) * C], posb[:, 1, c * P:(c + 1) * P], pw[:, c, :],
                              start=True, stop=True)
                last.then_inc(m_done, 1)
                for j in (4, 5, 6):
                    denominators_split(b, j)
                spread_z(b, 0)
                spread_z(b, 1)
                denominators_split(b, 7)
                spread_z(b, 2)
                spread_z(b, 3)
                pe.wait_ge(ml_ready, b + 1)
                output(b, 0)
                spread_z(b, 4)
                pe.wait_ge(zt_step, 8 * b + 6)
                output(b, 1)
                pe.wait_ge(u_ready, NBLK * b + 4)
                output(b, 2)
                for t in range(GRP0, NBLK):
                    spread_z(b, t)
                    output(b, t - LAG)
                if not last_batch:
                    pe.wait_ge(u_ready, NBLK * (b + 1))
                    gn_group_mean(b + 1)
                output(b, NBLK - 2, lambda: None if last_batch else gn_group_var(b + 1))
                output(b, NBLK - 1)

            with pe.Fori(0, B - 1) as b:
                batch(b, False)
            batch(B - 1, True)

        @block.vector
        def _(dve):
            v = nc.vector

            def x_stats(b, t, n):
                for c in range(CC):
                    last = v.bn_stats(stats[:, c, t, :], ring[:, slot(b, t), c, 0:n])
                last.then_inc(stats_done, 1)

            def gn_channels(b):
                dve.wait_ge(stats_done, NBLK * (b + 1))
                v.tensor_copy(landing[:], stats[:, 0, 0, 0:2])
                for c in range(CC):
                    last = v.bn_aggr(mv[:, c, :], stats[:, c, :, :].rearrange("p t s -> p (t s)"))
                last.then_inc(gn_step, 1)

            def gn_offsets(b):
                dve.wait_ge(gn_mean, b + 1)
                dve.wait_ge(gn_step, 10 * b + 1)
                v.tensor_copy(gmean[:], psG[:, 0, 0:CC])
                v.tensor_tensor(gdev[:], mv[:, :, 0], psG[:, 0, 0:CC], ALU.subtract).then_inc(gn_step, 1)
                dve.wait_ge(gn_step, 10 * b + 2)
                v.tensor_tensor(gtmp[:], gdev[:], gdev[:], ALU.mult).then_inc(gn_step, 1)
                dve.wait_ge(gn_step, 10 * b + 3)
                v.tensor_tensor(gvar[:], gtmp[:], mv[:, :, 1], ALU.add).then_inc(gn_step, 1)

            def gn_rstd(b):
                dve.wait_ge(gn_var, b + 1)
                v.tensor_scalar(gvar[:], psG[:, 0, 0:CC], GN_EPS, None, ALU.add).then_inc(gn_step, 1)
                dve.wait_ge(gn_sqrt, b + 1)
                v.reciprocal(rstd[:], gtmp[:]).then_inc(gn_step, 1)
                dve.wait_ge(gn_step, 10 * b + 6)
                v.tensor_tensor(gdev[:], rstd[:], rstd[:], ALU.mult).then_inc(gn_step, 1)
                dve.wait_ge(gn_step, 10 * b + 7)
                v.tensor_tensor(gdev[:], gdev[:], gvar[:], ALU.mult).then_inc(gn_step, 1)
                dve.wait_ge(gn_step, 10 * b + 8)
                v.tensor_scalar(gdev[:], gdev[:], -0.5, 1.5, ALU.mult, ALU.add).then_inc(gn_step, 1)
                dve.wait_ge(gn_step, 10 * b + 9)
                v.tensor_tensor(rstd[:], rstd[:], gdev[:], ALU.mult).then_inc(gn_step, 1)
                dve.wait_ge(gn_step, 10 * b + 10)

            def normalise(b, t, h, hp, tok):
                n = NHB * b + h
                if isinstance(h, int) and h == 0:
                    if not (isinstance(b, int) and b == 0):
                        dve.wait_ge(t_done, PRIME + n)
                        dve.wait_ge(xh_ready, PRIME + n)
                        dve.wait_ge(xl_ready, PRIME + n)
                else:
                    dve.wait_ge(t_done, PRIME + n - 1)
                    dve.wait_ge(xh_ready, PRIME + n - 1)
                    dve.wait_ge(xl_ready, PRIME + n - 1)
                for c in range(CC):
                    last = v.tensor_scalar(xn[:, hp, c, :], ring[:, slot(b, t), c, tok:tok + HALF],
                                           gmean[:, c:c + 1], rstd[:, c:c + 1], ALU.subtract, ALU.mult)
                last.then_inc(xn_ready, 1)

            def key_rest(b, h, hp, between=lambda: None):
                n = NHB * b + h
                dve.wait_ge(pos_loaded, 16 * (n + 1))
                if isinstance(b, int) and b == 0:
                    both = posb[:, hp, :].rearrange("p (i n) -> p i n", i=TILES)
                    v.tensor_tensor(both, both, bk_b, ALU.add).then_inc(pos_added, 1)
                    dve.wait_ge(pos_added, h + 1)
                dve.wait_ge(k_done, n + 1)
                dve.wait_ge(kacc_done, PRIME + n)
                dve.wait_ge(kl_ready, PRIME + n)
                v.tensor_tensor(kt[:], psK[:, hp, :], posb[:, hp, :], ALU.add).then_inc(kt_ready, 1)
                dve.wait_ge(xth_ready, n + 1)
                v.tensor_tensor(xt[:, hp, 1, :, :].rearrange("p i n -> p (i n)"), psT[:, hp, :],
                                xt[:, hp, 0, :, :].rearrange("p i n -> p (i n)"), ALU.subtract).then_inc(xtl_ready, 1)
                between()
                dve.wait_ge(kh_ready, n + 1)
                v.tensor_tensor(kk[:, hp, :, 1, :], kt[:].rearrange("p (i n) -> p i n", i=TILES), kk[:, hp, :, 0, :],
                                ALU.subtract).then_inc(kl_ready, 1)

            def add_parts(b):
                dve.wait_ge(zt_step, 8 * b + 5)
                for half, r in ((1, slice(64, 128)), (0, slice(0, 64))):
                    d = slice(half * HALF, (half + 1) * HALF)
                    last = v.scalar_tensor_tensor(out=kt[r, 0:HALF], in0=psT[0:64, 1, d], scalar=zeps[0:64, 0:1],
                                                  in1=kt[0:64, d], op0=ALU.add, op1=ALU.add)
                last.then_inc(zt_step, 1)

            def invert(b, g):
                dve.wait_ge(zt_step, 8 * b + (6 if g else 2))
                v.reciprocal(kt[:, 0:HALF], kt[:, 0:HALF]).then_inc(zt_step, 1)

            def z_low(b, g):
                dve.wait_ge(zh_ready, 2 * b + g + 1)
                v.tensor_tensor(zhl[64:128, g, :], kt[0:64, :], zhl[0:64, g, :], ALU.subtract).then_inc(zl_ready, 1)

            def q_low(b):
                j = LOW_BY_DVE
                dve.wait_ge(qh_ready, GRP1 * b + j + 1)
                v.tensor_tensor(ubuf[j % 3][:, 1, :, :], q[:, :, cols(GRP0 + j, BLK)], ubuf[j % 3][:, 0, :, :],
                                ALU.subtract).then_inc(ql_dve, 1)

            def scale_q(b, t, n):
                dve.wait_ge(zb_done, NBLK * b + t + 1)
                v.tensor_tensor(q[:, :, cols(t, n)], q[:, :, cols(t, n)], z_bank(t)[:, :, 0:n], ALU.mult).then_inc(u_ready, 1)

            def residual(b, t, n, psO, chunks):
                for m in chunks:
                    dve.wait_ge(o_done, PRIME + CC * (NBLK * b + t) + m + 1)
                    xs = ring[:, slot(b, t), m, 0:n]
                    v.scalar_tensor_tensor(out=xs, in0=psO[:, m, 0:n], scalar=pb[:, m:m + 1], in1=xs,
                                           op0=ALU.add, op1=ALU.add).then_inc(out_ready, 1)

            v.memset(ones[:], 1.0)
            v.memset(zeps[:], Z_EPS)
            v.memset(kacc[:], 0.0).then_inc(kacc_zero, 1)
            v.memset(swin[:], 0.0)
            v.memset(swr[:].bitcast(F32), 0.0)
            for t in range(4):
                dve.wait_ge(x_first[t % 4], 16)
                x_stats(0, t, BLK if t else HEAD)
            dve.wait_ge(w_loaded, 16 * 13)
            for c in range(CC):
                last = v.tensor_scalar(bvm[:, c, :], bmask, bv[:, c:c + 1], None, ALU.mult)
            last.then_inc(bvm_ready, 1)
            v.tensor_copy(esel[:], esel_raw)
            v.tensor_copy(wqk[:, 0, :, :], wqk_raw).then_inc(w_high, 1)
            dve.wait_ge(w_high, 1)
            v.tensor_tensor(wqk[:, 1, :, :], wqk_raw, wqk[:, 0, :, :], ALU.subtract)
            for t in range(4, NBLK):
                dve.wait_ge(x_first[t % 4], 16 * (t // 4 + 1))
                x_stats(0, t, BLK)
            dve.wait_ge(bpb_done, 1)
            v.tensor_copy(bpb[:].rearrange("p c n -> p (c n)"), psK[:, 0, :]).then_inc(setup_done, 1)
            gn_channels(0)
            gn_offsets(0)
            gn_rstd(0)
            normalise(0, 0, 0, 0, 0)
            normalise(0, 1, 1, 1, 0)

            def batch(b, last_batch):
                def pair(t, with_stats):
                    key_rest(b, 2 * t - 2, 0, lambda: normalise(b, t, 2 * t, 0, HALF))
                    if isinstance(t, int) and t == NBLK - 1:
                        key_rest(b, 2 * t - 1, 1)
                    else:
                        key_rest(b, 2 * t - 1, 1, lambda: normalise(b, t + 1, 2 * t + 1, 1, 0))
                    if with_stats:
                        dve.wait_ge(x_loaded, PRIME_DMA + 16 * (NBLK * b + t - NBLK + EARLY + 1))
                        x_stats(b + 1, t - NBLK + EARLY, BLK)
                if isinstance(b, int) and b == 0:
                    for t in range(1, NBLK):
                        pair(t, t > NBLK - EARLY)
                        if t == NBLK - EARLY:
                            dve.wait_ge(x_loaded, PRIME_DMA + 16)
                            x_stats(1, 0, HEAD)
                else:
                    with dve.Fori(0, 2) as i:
                        pair(2 * i + 1, False)
                        pair(2 * i + 2, False)
                    if not last_batch:
                        dve.wait_ge(x_loaded, PRIME_DMA + 16 * (NBLK * b + 1))
                        x_stats(b + 1, 0, HEAD)
                    with dve.Fori(2, 5) as i:
                        pair(2 * i + 1, not last_batch)
                        pair(2 * i + 2, not last_batch)
                    pair(NBLK - 2, not last_batch)
                    pair(NBLK - 1, not last_batch)
                key_rest(b, NHB - 1, 0)
                kvm = posb[:, 1, 0:CC * P].rearrange("p (c n) -> p c n", c=CC)
                kvt = psK[:, 1, 0:CC * P].rearrange("p (c n) -> p c n", c=CC)
                if isinstance(b, int) and b == 0:
                    dve.wait_ge(pos_stored, 16 * (NHB - 1))
                v.memset(kvm, 0.0).then_inc(kvm_zero, 1)
                dve.wait_ge(ksum_done, b + 1)
                v.tensor_copy(ksc[:], psK[:, 0, 0:CC]).then_inc(ksc_ready, 1)
                dve.wait_ge(ksc_ready, b + 1)
                for c in range(CC):
                    s = WIN0 + 32 * c
                    last = v.tensor_scalar(swin[:, c, s:s + HPC], hmask[:], ksc[:, c:c + 1], None, ALU.mult)
                last.then_inc(swin_ready, 1)
                for c in range(CC):
                    s = WIN1 + 32 * c
                    last = v.tensor_scalar(swr[:, c, s:s + HPC], hmask[:], ksc[:, c:c + 1], None, ALU.mult)
                last.then_inc(swr_step, 1)
                dve.wait_ge(swin_ready, b + 1)
                dve.wait_ge(swr_step, 2 * b + 1)
                for c in range(CC):
                    s, f = WIN1 + 32 * c, WIN0 + 32 * c
                    last = v.tensor_tensor(swr[:, c, s + 64:s + 64 + HPC], swin[:, c, f:f + HPC], swr[:, c, s:s + HPC],
                                           ALU.subtract)
                last.then_inc(swr_step, 1)
                v.memset(kacc[:], 0.0).then_inc(kacc_zero, 1)
                gt = posb[:, 0, :].rearrange("p (c n) -> p c n", c=CC)
                dve.wait_ge(gl_copied, b + 1)
                v.tensor_tensor(gt, psG[:, :, 0:C], gt, ALU.add).then_inc(gt_ready, 1)
                q_low(b)
                dve.wait_ge(kv_done, b + 1)
                dve.wait_ge(kvm_zero, b + 1)
                for h in range(HPC):
                    d = slice(h * HD, (h + 1) * HD)
                    last = v.tensor_copy(kvm[d, :, d], kvt[d, :, d])
                last.then_inc(kvm_ready, 1)
                invert(b, 0)
                dve.wait_ge(m_done, b + 1)
                for c in range(CC):
                    last = v.scalar_tensor_tensor(out=posb[:, 0, c * C:(c + 1) * C], in0=bpb[:, c, :], scalar=ksc[:, c:c + 1],
                                                  in1=psQ[:, 0, c * C:(c + 1) * C], op0=ALU.mult, op1=ALU.add)
                last.then_inc(m_sum, 1)
                z_low(b, 0)
                dve.wait_ge(mh_ready, b + 1)
                v.tensor_tensor(mhl[:, 1, :, :].rearrange("p c n -> p (c n)"), posb[:, 0, :],
                                mhl[:, 0, :, :].rearrange("p c n -> p (c n)"), ALU.subtract).then_inc(ml_ready, 1)
                scale_q(b, 0, HEAD)
                scale_q(b, 1, BLK)
                add_parts(b)
                scale_q(b, 2, BLK)
                invert(b, 1)
                scale_q(b, 3, BLK)
                scale_q(b, 4, BLK)
                z_low(b, 1)
                def out_block(t, chunks=range(CC)):
                    residual(b, t, BLK if t else HEAD, out_banks[t % 3], chunks)

                for t in range(GRP0 - LAG - 1):
                    out_block(t)
                for t in range(GRP0, NBLK):
                    scale_q(b, t, BLK)
                    if t == NBLK - 1 and not last_batch:
                        gn_channels(b + 1)
                        out_block(t - LAG - 1, [0])
                        gn_offsets(b + 1)
                        out_block(t - LAG - 1, [1])
                    else:
                        out_block(t - LAG - 1)
                    for i in [i for i in range(len(STATS_AT)) if STATS_AT[i] == t and not last_batch]:
                        k = EARLY + i // CC
                        if i % CC == 0:
                            dve.wait_ge(x_loaded, PRIME_DMA + 16 * (NBLK * b + k + 1))
                        last = v.bn_stats(stats[:, i % CC, k, :], ring[:, slot(b + 1, k), i % CC, :])
                        if i % CC == CC - 1:
                            last.then_inc(stats_done, 1)
                if not last_batch:
                    gn_rstd(b + 1)
                    normalise(b + 1, 0, 0, 0, 0)
                out_block(NBLK - 3)
                out_block(NBLK - 2)
                if not last_batch:
                    normalise(b + 1, 1, 1, 1, 0)
                out_block(NBLK - 1)

            batch(0, False)
            with dve.Fori(1, B - 1) as b:
                batch(b, False)
            batch(B - 1, True)

        @block.scalar
        def _(act):
            a = nc.scalar.activation

            def gn_root(b):
                act.wait_ge(gn_step, 10 * b + 5)
                a(gtmp[:], gvar[:], ACT.Sqrt).then_inc(gn_sqrt, 1)

            def xn_high(b, h, par, hp, tok, free):
                act.wait_ge(xn_ready, NHB * b + h + 1)
                free(act)
                a(hl[:, par, 0, :, tok:tok + HALF], xn[:, hp, :, :], ACT.Copy).then_inc(xh_ready, 1)

            def rest(b, h, hp):
                n = NHB * b + h
                act.wait_ge(t_done, PRIME + n + 1)
                if isinstance(h, int) and h == 0:
                    act.wait_ge(g_done, PRIME + n)
                else:
                    act.wait_ge(g_done, PRIME + n - 1)
                a(xt[:, hp, 0, :, :].rearrange("p i n -> p (i n)"), psT[:, hp, :], ACT.Copy).then_inc(xth_ready, 1)
                act.wait_ge(kt_ready, PRIME + n + 1)
                a(kt[:], kt[:], ACT.Relu).then_inc(kr_ready, 1)
                act.wait_ge(kr_ready, n + 1)
                a(kk[:, hp, :, 0, :], kt[:].rearrange("p (i n) -> p i n", i=TILES), ACT.Copy).then_inc(kh_ready, 1)

            def save_q(b, t, n, m):
                act.wait_ge(q_done, CC * (NBLK * b + t) + m + 1)
                a(q[:, m, cols(t, n)], psQ[:, m, 0:n], ACT.Relu, bias=bq[:, m:m + 1]).then_inc(q_saved, 1)

            def block_free(b, t):
                return lambda eng: eng.wait_ge(q_done, CC * (NBLK * b + t - 1))

            def phase_free(b, k):
                return lambda eng: eng.wait_ge(o_done, PRIME + CC * (NBLK * b + k))

            def q_high(b, j, free):
                t = GRP0 + j
                act.wait_ge(q_saved, CC * (NBLK * b + t + 1))
                if j < 3:
                    free()
                else:
                    act.wait_ge(qs_used, GRP1 * b + j - 2)
                a(ubuf[j % 3][:, 0, :, :], q[:, :, cols(t, BLK)], ACT.Copy).then_inc(qh_ready, 1)

            def z_eps(b):
                act.wait_ge(den_done, b + 1)
                a(kt[0:64, 0:HALF], psT[0:64, 0, 0:HALF], ACT.Identity, bias=zeps[0:64, 0:1]).then_inc(zt_step, 1)
                a(kt[64:128, 0:HALF], psT[0:64, 0, HALF:BLK], ACT.Identity, bias=zeps[0:64, 0:1]).then_inc(zt_step, 1)

            def low_rows(b):
                act.wait_ge(qs_used, GRP1 * (b + 1))
                act.wait_ge(zl_ready, 2 * b + 1)
                a(kt[0:64, :], psT[64:128, 1, :], ACT.Copy).then_inc(zt_step, 1)

            def z_high(b, g):
                done = 8 * b + (7 if g else 3)
                act.wait_ge(zt_step, done)
                a(kt[0:64, HALF:BLK], kt[64:128, 0:HALF], ACT.Copy).then_inc(zt_step, 1)
                act.wait_ge(zt_step, done + 1)
                a(zhl[0:64, g, :], kt[0:64, :], ACT.Copy).then_inc(zh_ready, 1)

            def u_high(b, t, n, buf):
                act.wait_ge(u_ready, NBLK * b + t + 1)
                if t < 3:
                    act.wait_ge(qs_used, GRP1 * b + (7, 8, 6)[t])
                else:
                    act.wait_ge(o_done, PRIME + CC * (NBLK * b + t - 2))
                a(ubuf[buf][:, 0, :, 0:n], q[:, :, cols(t, n)], ACT.Copy).then_inc(uh_ready, 1)

            gn_root(0)
            xn_high(0, 0, 1, 0, 0, lambda eng: None)

            def batch(b, last_batch):
                xn_high(b, 1, 0, 1, 0, phase_free(b, 0))
                rest(b, 0, 0)

                def step(t, par):
                    xn_high(b, 2 * t, par, 0, HALF, lambda eng: None)
                    if isinstance(t, int) and t == 1:
                        save_q(b, 0, HEAD, 0)
                        save_q(b, 0, HEAD, 1)
                    rest(b, 2 * t - 1, 1)
                    save_q(b, t, BLK, 0)
                    xn_high(b, 2 * t + 1, 1 - par, 1, 0, block_free(b, t + 1))
                    rest(b, 2 * t, 0)
                    save_q(b, t, BLK, 1)
                step(1, 0)
                with act.Fori(0, 5) as i:
                    step(2 * i + 2, 1)
                    step(2 * i + 3, 0)
                xn_high(b, NHB - 1, 1, 0, HALF, lambda eng: None)
                rest(b, NHB - 2, 1)
                q_high(b, 0, lambda: act.wait_ge(q_done, CC * (NBLK * b + NBLK - 1)))
                rest(b, NHB - 1, 0)
                save_q(b, NBLK - 1, BLK, 0)
                save_q(b, NBLK - 1, BLK, 1)
                q_high(b, 1, lambda: act.wait_ge(q_done, CC * NBLK * (b + 1)))
                act.wait_ge(g_done, PRIME + NHB * (b + 1))
                act.wait_ge(kt_ready, PRIME + NHB * (b + 1))
                act.wait_ge(pos_stored, 16 * NHB)
                a(posb[:, 0, :].rearrange("p (c n) -> p c n", c=CC), psG[:, :, C:2 * C], ACT.Copy).then_inc(gl_copied, 1)
                q_high(b, 2, lambda: act.wait_ge(g_done, PRIME + NHB * (b + 1)))
                q_high(b, 3, None)
                q_high(b, 4, None)
                q_high(b, 5, None)
                q_high(b, 6, None)
                z_eps(b)
                q_high(b, 7, None)
                z_high(b, 0)
                act.wait_ge(m_sum, b + 1)
                a(mhl[:, 0, :, :].rearrange("p c n -> p (c n)"), posb[:, 0, :], ACT.Copy).then_inc(mh_ready, 1)
                low_rows(b)
                u_high(b, 0, HEAD, 0)
                u_high(b, 1, BLK, 1)
                u_high(b, 2, BLK, 2)
                z_high(b, 1)
                for t in range(3, NBLK):
                    u_high(b, t, BLK, t % 3)
                if not last_batch:
                    gn_root(b + 1)
                    xn_high(b + 1, 0, 1, 0, 0, phase_free(b, NBLK - 2))

            with act.Fori(0, B - 1) as b:
                batch(b, False)
            batch(B - 1, True)

        @block.gpsimd
        def _(pool):
            g = nc.gpsimd

            def xn_low(b, h, par, hp, tok):
                pool.wait_ge(xh_ready, PRIME + NHB * b + h + 1)
                g.tensor_tensor(hl[:, par, 1, :, tok:tok + HALF], xn[:, hp, :, :], hl[:, par, 0, :, tok:tok + HALF],
                                ALU.subtract).then_inc(xl_ready, 1)

            def key_sum(b, h):
                n = NHB * b + h
                pool.wait_ge(kr_ready, n + 1)
                pool.wait_ge(kacc_zero, b + 1)
                pool.wait_ge(kacc_done, PRIME + n)
                g.tensor_tensor(kacc[:].rearrange("p i n -> p (i n)"), kacc[:].rearrange("p i n -> p (i n)"), kt[:],
                                ALU.add).then_inc(kacc_done, 1)

            def u_low(b, t, n, buf):
                pool.wait_ge(uh_ready, NBLK * b + t + 1)
                g.tensor_tensor(ubuf[buf][:, 1, :, 0:n], q[:, :, cols(t, n)], ubuf[buf][:, 0, :, 0:n],
                                ALU.subtract).then_inc(ul_ready, 1)

            def q_low(b, j):
                pool.wait_ge(qh_ready, GRP1 * b + j + 1)
                g.tensor_tensor(ubuf[j % 3][:, 1, :, :], q[:, :, cols(GRP0 + j, BLK)], ubuf[j % 3][:, 0, :, :],
                                ALU.subtract).then_inc(ql_ready, 1)

            for s in primed:
                pool.sem_inc(s, PRIME)
            for s in primed_dma:
                pool.sem_inc(s, PRIME_DMA)
            xn_low(0, 0, 1, 0, 0)

            def batch(b, last_batch):
                with pool.Fori(0, 6) as i:
                    for s in (1, 2):
                        t = 2 * i + s
                        par = (s + 1) % 2
                        xn_low(b, 2 * t - 1, par, 1, 0)
                        key_sum(b, 2 * t - 2)
                        xn_low(b, 2 * t, par, 0, HALF)
                        key_sum(b, 2 * t - 1)
                q_low(b, 0)
                key_sum(b, NHB - 1)
                for j in range(1, GRP1):
                    if j != LOW_BY_DVE:
                        q_low(b, j)
                u_low(b, 0, HEAD, 0)
                with pool.Fori(0, 4) as i:
                    for s in (1, 2, 3):
                        u_low(b, 3 * i + s, BLK, s % 3)
                if not last_batch:
                    xn_low(b + 1, 0, 1, 0, 0)

            with pool.Fori(0, B - 1) as b:
                batch(b, False)
            batch(B - 1, True)


def kernel(**inputs):
    import concourse.bacc as bacc
    from concourse.bass_utils import run_bass_kernel_spmd

    x = np.ascontiguousarray(inputs["x"])
    qkv_w = np.asarray(inputs["L0_conv_qkv_w"])
    qkv_b = np.asarray(inputs["L0_conv_qkv_b"])
    proj_w = np.asarray(inputs["L0_conv_proj_w"])
    proj_b = np.asarray(inputs["L0_conv_proj_b"])
    chan = np.arange(P)
    same_head = (chan[:, None] // HD == chan[None, :] // HD)
    row = 32 * np.arange(CC)[None, :, None] + 4 * np.arange(GRP1)[:, None, None] + (chan // HD)[None, None, :]
    esel = (np.arange(P)[:, None, None, None] % 64 == row[None]).reshape(P, GRP1 * CC, P)
    arrays = {
        "x": x.reshape(B, CC, P, N),
        "wqk": np.ascontiguousarray(qkv_w[:2 * C].T).reshape(CC, P, 2 * C),
        "wv": np.ascontiguousarray(qkv_w[2 * C:].T).reshape(CC, P, C),
        "pw": np.ascontiguousarray(proj_w.T).reshape(CC, P, C),
        "bq": np.ascontiguousarray(qkv_b[:C].reshape(CC, P).T),
        "bk": np.ascontiguousarray(qkv_b[C:2 * C].reshape(1, C)),
        "bv": np.ascontiguousarray(qkv_b[2 * C:].reshape(CC, P).T),
        "pb": np.ascontiguousarray(proj_b.reshape(CC, P).T),
        "pos": np.ascontiguousarray(
            np.asarray(inputs["L0_conv_pos_enc"]).reshape(NHB, TILES, P, C).transpose(0, 2, 1, 3)).reshape(NHB, P, TILES * C),
        "ident": np.eye(P, dtype=np.float32),
        "gavg": (chan[:, None] // GROUP == chan[None, :] // GROUP).astype(np.float32) / GROUP,
        "hmask": (chan[:, None] // HD == np.arange(HPC)[None, :]).astype(np.float32),
        "bmask": same_head.astype(np.float32),
        "esel": esel.astype(np.float32),
    }
    arrays = {f"in_{name}": a for name, a in arrays.items()}
    nc = bacc.Bacc("TRN2", target_bir_lowering=False, num_devices=1)
    f32 = mybir.dt.float32
    args = [nc.dram_tensor(name, a.shape, f32, kind="ExternalInput").ap() for name, a in arrays.items()]
    posb = nc.dram_tensor("pos_plus_bk", (NHB, P, TILES * C), f32, kind="Internal").ap()
    y = nc.dram_tensor("y", (B, CC, P, N), f32, kind="ExternalOutput").ap()
    build(nc, *args, posb, y)
    r = run_bass_kernel_spmd(nc, [arrays], core_ids=[0])
    return r.results[0]["y"].reshape(B, C, H, W)
```
